# Optimizing a Trainium2 kernel written in Bass

```python
import numpy as np
import jax
import jax.numpy as jnp

def _softmax(x, axis=-1):
    return jax.nn.softmax(x, axis=axis)

def _gelu(x):
    return jax.nn.gelu(x, approximate=True)

def _silu(x):
    return jax.nn.silu(x)

def _sigmoid(x):
    return jax.nn.sigmoid(x)

def _layernorm(x, axis=-1, eps=1e-05):
    m = jnp.mean(x, axis=axis, keepdims=True)
    v = jnp.var(x, axis=axis, keepdims=True)
    return (x - m) / jnp.sqrt(v + eps)

def _scatter_add(tgt, idx, src, axis=0):
    return tgt.at[idx].add(src)

def _segment_sum(src, seg, n):
    return jax.ops.segment_sum(src, seg, n)
kernel_name = 'mk_seq_preln_d1_jaxref_r4_2f3dc3'

def setup_inputs(seed: int=0):
    np.random.seed(seed)
    _w = jnp.asarray

    def _L0_attn_setup():
        import jax, jax.numpy as jnp
        import numpy as np
        D_MODEL, D_HIDDEN = (256, 512)
        B, L = (4, 1024)

        def _lin(x, w, b=None):
            y = jnp.einsum('bld,od->blo', x, w)
            return y if b is None else y + b

        def _depthwise_conv(x, conv_w, conv_b):
            lhs = jnp.transpose(x, (0, 2, 1))
            y = jax.lax.conv_general_dilated(lhs, conv_w, window_strides=(1,), padding=[(1, 1)], dimension_numbers=('NCH', 'OIH', 'NCH'), feature_group_count=D_MODEL)
            y = y + conv_b[None, :, None]
            return jnp.transpose(y, (0, 2, 1))
        key = jax.random.key(seed)
        ks = jax.random.split(key, 16)
        r = lambda k, shape, s: s * jax.random.normal(k, shape, dtype=jnp.float32)
        inp = {'x': r(ks[0], (B, L, D_MODEL), 1.0), 'w1': r(ks[1], (D_MODEL, D_MODEL), 0.02), 'w2': r(ks[2], (D_MODEL, D_MODEL), 0.02), 'w3': r(ks[3], (D_MODEL, D_MODEL), 0.02), 'conv_w': r(ks[4], (D_MODEL, 1, 3), 0.1), 'conv_b': r(ks[5], (D_MODEL,), 0.02), 'A_w': r(ks[6], (D_HIDDEN, D_MODEL), 0.001), 'A_b': jnp.ones((D_HIDDEN,), jnp.float32), 'B_w': r(ks[7], (D_HIDDEN, D_MODEL), 0.02), 'B_b': jnp.zeros((D_HIDDEN,), jnp.float32), 'C_w': r(ks[8], (D_MODEL, D_HIDDEN), 0.02), 'C_b': jnp.zeros((D_MODEL,), jnp.float32), 'D_w': r(ks[9], (D_MODEL, D_MODEL), 0.02), 'D_b': jnp.zeros((D_MODEL,), jnp.float32), 'dl_w': r(ks[10], (D_HIDDEN, D_MODEL), 0.001), 'dl_b': -5.0 * jnp.ones((D_HIDDEN,), jnp.float32)}
        return inp
    _L0_attn_in = _L0_attn_setup()

    def _L0_ffn_setup():
        import jax, jax.numpy as jnp
        import numpy as np
        LN_EPS = 0.001
        EPS = 1e-05
        QB = 128.0

        def ste_round(x):
            return x + jax.lax.stop_gradient(jnp.round(x) - x)
        key = jax.random.key(seed)
        k1, k2 = jax.random.split(key)
        x = jax.random.normal(k1, (4, 2048, 256), dtype=jnp.float32)
        weight = jax.random.normal(k2, (256, 256), dtype=jnp.float32) * 0.02
        ln_gamma = jnp.ones((256,), dtype=jnp.float32)
        ln_beta = jnp.zeros((256,), dtype=jnp.float32)
        return {'x': x, 'weight': weight, 'ln_gamma': ln_gamma, 'ln_beta': ln_beta}
    _L0_ffn_in = _L0_ffn_setup()
    _d = {'L0_attn_x': _L0_attn_in['x'], 'L0_attn_w1': _L0_attn_in['w1'], 'L0_attn_w2': _L0_attn_in['w2'], 'L0_attn_w3': _L0_attn_in['w3'], 'L0_attn_conv_w': _L0_attn_in['conv_w'], 'L0_attn_conv_b': _L0_attn_in['conv_b'], 'L0_attn_A_w': _L0_attn_in['A_w'], 'L0_attn_A_b': _L0_attn_in['A_b'], 'L0_attn_B_w': _L0_attn_in['B_w'], 'L0_attn_B_b': _L0_attn_in['B_b'], 'L0_attn_C_w': _L0_attn_in['C_w'], 'L0_attn_C_b': _L0_attn_in['C_b'], 'L0_attn_D_w': _L0_attn_in['D_w'], 'L0_attn_D_b': _L0_attn_in['D_b'], 'L0_attn_dl_w': _L0_attn_in['dl_w'], 'L0_attn_dl_b': _L0_attn_in['dl_b'], 'L0_ffn_weight': _L0_ffn_in['weight'], 'L0_ffn_ln_gamma': _L0_ffn_in['ln_gamma'], 'L0_ffn_ln_beta': _L0_ffn_in['ln_beta']}
    _x0 = _d['L0_attn_x']
    _d['L0_attn_x'] = jax.random.normal(jax.random.fold_in(jax.random.key(seed), 1), (32, 512, 256), dtype=_x0.dtype)
    del _x0
    return _d

def reference(L0_attn_x, L0_attn_w1, L0_attn_w2, L0_attn_w3, L0_attn_conv_w, L0_attn_conv_b, L0_attn_A_w, L0_attn_A_b, L0_attn_B_w, L0_attn_B_b, L0_attn_C_w, L0_attn_C_b, L0_attn_D_w, L0_attn_D_b, L0_attn_dl_w, L0_attn_dl_b, L0_ffn_weight, L0_ffn_ln_gamma, L0_ffn_ln_beta):

    def _L0_attn_ref(x, w1, w2, w3, conv_w, conv_b, A_w, A_b, B_w, B_b, C_w, C_b, D_w, D_b, dl_w, dl_b):
        import jax, jax.numpy as jnp
        import numpy as np
        D_MODEL, D_HIDDEN = (256, 512)
        B, L = (4, 1024)

        def _lin(x, w, b=None):
            y = jnp.einsum('bld,od->blo', x, w)
            return y if b is None else y + b

        def _depthwise_conv(x, conv_w, conv_b):
            lhs = jnp.transpose(x, (0, 2, 1))
            y = jax.lax.conv_general_dilated(lhs, conv_w, window_strides=(1,), padding=[(1, 1)], dimension_numbers=('NCH', 'OIH', 'NCH'), feature_group_count=D_MODEL)
            y = y + conv_b[None, :, None]
            return jnp.transpose(y, (0, 2, 1))
        x = _lin(x, w1)
        x = _depthwise_conv(x, conv_w, conv_b)
        x = jax.nn.silu(x)
        x_delta = jax.nn.softplus(_lin(x, dl_w, dl_b))
        A_t = _lin(x, A_w, A_b)
        A_bar = jnp.exp(-x_delta * A_t)
        B_x = _lin(x, B_w, B_b)
        A_cum = jnp.cumprod(A_bar, axis=1)
        h = jnp.cumsum(B_x * A_cum, axis=1)
        ssm_out = _lin(h, C_w, C_b) + _lin(x, D_w, D_b)
        x_res = jax.nn.silu(_lin(ssm_out, w2))
        z = ssm_out * x_res
        out = ssm_out + _lin(z, w3)
        return out

    def _L0_ffn_ref(x, weight, ln_gamma, ln_beta):
        import jax, jax.numpy as jnp
        import numpy as np
        LN_EPS = 0.001
        EPS = 1e-05
        QB = 128.0

        def ste_round(x):
            return x + jax.lax.stop_gradient(jnp.round(x) - x)
        mu = jnp.mean(x, axis=-1, keepdims=True)
        var = jnp.var(x, axis=-1, keepdims=True)
        xn = (x - mu) * jax.lax.rsqrt(var + LN_EPS) * ln_gamma + ln_beta
        beta = jnp.mean(jnp.abs(weight))
        w_q = jnp.clip(ste_round(weight / (beta + EPS)), -1.0, 1.0)
        gamma = jnp.max(jnp.abs(xn))
        xq = jnp.clip(xn * QB / gamma, -QB + EPS, QB - EPS)
        y = jnp.einsum('bsd,du->bsu', xq, w_q)
        return y * (gamma * beta / QB)
    x = L0_attn_x
    x = x + _L0_attn_ref(_layernorm(x, axis=-1), L0_attn_w1, L0_attn_w2, L0_attn_w3, L0_attn_conv_w, L0_attn_conv_b, L0_attn_A_w, L0_attn_A_b, L0_attn_B_w, L0_attn_B_b, L0_attn_C_w, L0_attn_C_b, L0_attn_D_w, L0_attn_D_b, L0_attn_dl_w, L0_attn_dl_b)
    x = x + _L0_ffn_ref(_layernorm(x, axis=-1), L0_ffn_weight, L0_ffn_ln_gamma, L0_ffn_ln_beta)
    return x

_drawn_inputs = setup_inputs


def setup_inputs(seed=0):
    import zlib

    import numpy as np

    out = dict(_drawn_inputs(seed))
    spreads = {'L0_attn_A_b': (1.0, 0.2),
     'L0_attn_B_b': (0.0, 0.1),
     'L0_attn_C_b': (0.0, 2.0),
     'L0_attn_D_b': (0.0, 2.0),
     'L0_attn_dl_b': (-5.0, 0.2),
     'L0_ffn_ln_gamma': (1.0, 0.6),
     'L0_ffn_ln_beta': (0.0, 2.0)}
    factors = {'L0_attn_w1': 8.0,
     'L0_attn_conv_w': 8.0,
     'L0_attn_A_w': 8.0,
     'L0_attn_D_w': 8.0,
     'L0_attn_dl_w': 8.0,
     'L0_attn_conv_b': 5.687,
     'L0_ffn_weight': 8.0}
    for name, (base, spread) in spreads.items():
        noise = np.random.default_rng([zlib.crc32(name.encode()), seed]).standard_normal(out[name].shape)
        drawn = base * np.exp(spread * noise) if base else spread * noise
        out[name] = jnp.asarray(drawn.astype(out[name].dtype))
    for name, factor in factors.items():
        out[name] = (out[name] * factor).astype(out[name].dtype)
    return out
```

```python
from contextlib import ExitStack

import numpy as np

import concourse.bass as bass
from concourse import mybir

P = 128
F32 = mybir.dt.float32
F32R = mybir.dt.float32r
ALU = mybir.AluOpType
ACT = mybir.ActivationFunctionType
AX = mybir.AxisListType

LN_EPS = 1e-5
FFN_LN_EPS = 1e-3
QB = 128.0
Q_EPS = 1e-5
CLIP = float(np.float32(QB - Q_EPS))
ROUND_MAGIC = 1.5 * 2.0**23
EXP_CAP = 2.0**62
BIG = 3.0e38

EXP_LN_TABLE = "natural_log_exp_and_others"
SILU_TABLE = "silu_and_others"


def column_layout(D, H):
    at, where = 0, {}
    for name, n in [("dl_b", H // P), ("A_b", H // P), ("B_b", H // P), ("C_b", D // P), ("D_b", D // P),
                    ("conv_b", D // P), ("conv_w0", D // P), ("conv_w1", D // P), ("conv_w2", D // P),
                    ("ln_gamma", D // P), ("ln_beta", D // P)]:
        where[name] = at
        at += n
    return where, at


def build(nc, x, w1T, w2T, w3T, dlT, AT, BT, CT, DT, ffn_w, columns, gamma_row, beta_row, out):
    B, L, D = x.shape
    H = dlT.shape[1]
    CD = D // P
    HD = H // P
    TT = L // P
    XW = D + 2
    assert (CD, HD, TT) == (2, 4, 4) and L == 512 and B % 4 == 0 and B >= 12
    col_at, n_cols = column_layout(D, H)

    x_v = x.rearrange("b (t p) d -> b p t d", p=P)
    out_v = out.rearrange("b (t p) d -> b p t d", p=P)
    scratch = nc.dram_tensor("x1_scratch", [B, P, TT * XW], F32, kind="Internal").ap()

    with ExitStack() as ctx:
        def sb(name, shape, dt=F32):
            return ctx.enter_context(nc.sbuf_tensor(name, shape, dt))

        def sem(name):
            return ctx.enter_context(nc.semaphore(name))

        NAMES = [("w1", CD, D), ("dl", CD, H), ("A", CD, H), ("B", CD, H), ("C", HD, D), ("D", CD, D), ("w2", CD, D),
                 ("w3", CD, D)]
        w_hi = {n: sb(f"{n}_hi", [P, k, o], F32R) for n, k, o in NAMES}
        w_lo = {n: sb(f"{n}_lo", [P, k, o], F32R) for n, k, o in NAMES}
        wq = sb("wq", [P, CD, D], F32R)
        ident = sb("ident", [P, P])
        ident_r = sb("ident_r", [P, P], F32R)
        ones = sb("ones", [P, P])
        neg_half = sb("neg_half", [P, TT])
        cols = sb("cols", [P, n_cols])
        cd_b = sb("cd_b", [P, CD])
        g_row = sb("g_row", [P, D])
        b_row = sb("b_row", [P, D])
        hi_run = sb("hi_run", [P, TT, D])
        lo_run = sb("lo_run", [P, TT, D])
        scal = sb("scal", [P, 16])

        x_in = sb("x_in", [P, 2, TT, D])
        x_res = sb("x_res", [P, TT, D])
        x_stat = sb("x_stat", [P, TT, 6])
        x_mv = sb("x_mv", [P, TT, 2])
        x_rstd = sb("x_rstd", [P, TT])
        xn = sb("xn", [P, TT, D])
        xn_hi = sb("xn_hi", [P, CD, L], F32R)
        xn_lo = sb("xn_lo", [P, CD, L], F32R)
        xs = sb("xs", [P, CD, L])
        xs_hi = sb("xs_hi", [P, 2, CD, L], F32R)
        xs_lo = sb("xs_lo", [P, 2, CD, L], F32R)
        temps = sb("temps", [P, 10 * L])

        def temp(k):
            return temps[:, k * 2 * L:(k + 1) * 2 * L].rearrange("p (r l) -> p r l", r=2)

        softp, delta, cumul, gated, hsum = temp(0), temp(1), temp(2), temp(3), temp(4)
        h_hi = sb("h_hi", [P, 2, HD, L], F32R)
        h_lo = sb("h_lo", [P, 2, HD, L], F32R)
        s_buf = sb("s_buf", [P, CD, L])
        s_hi = sb("s_hi", [P, CD, L], F32R)
        s_lo = sb("s_lo", [P, CD, L], F32R)
        gate = sb("gate", [P, CD, L])
        z_buf = sb("z_buf", [P, CD, L])
        z_hi = sb("z_hi", [P, CD, L], F32R)
        z_lo = sb("z_lo", [P, CD, L], F32R)
        x1 = sb("x1", [P, 2, TT, XW])
        x1_stat = sb("x1_stat", [P, TT, 6])
        x1_mv = sb("x1_mv", [P, TT, 2])
        x1_tmp = sb("x1_tmp", [P, 2, TT])
        x1n = sb("x1n", [P, TT, D])

        stage_at, raw = 0, {}
        for name, k, o in NAMES:
            if name == "C":
                raw[name] = x1n[:, :, :].rearrange("p t d -> p (t d)").rearrange("p (k o) -> p k o", k=k)
            else:
                raw[name] = temps[:, stage_at:stage_at + k * o].rearrange("p (k o) -> p k o", k=k)
                stage_at += k * o
        assert stage_at <= 10 * L
        raw_ffn = s_buf

        R1 = 4
        x1_in = temps[:, 0:R1 * TT * XW].rearrange("p (r t d) -> p r t d", r=R1, t=TT)
        xn2 = x_in
        xc = [z_buf, gate]
        q_hi, q_lo = xs_hi, xs_lo
        y_out = [xn, x1n]

        hb = ctx.enter_context(nc.psum_tensor("hidden_banks", [P, 6, L], F32))
        mb = ctx.enter_context(nc.psum_tensor("misc_banks", [P, 2, L], F32))

        d_x = [sem(f"d_x{r}") for r in range(2)]
        d_store = [sem(f"d_store{r}") for r in range(2)]
        d_x1 = [sem(f"d_x1_{r}") for r in range(4)]
        d_out = [sem(f"d_out{r}") for r in range(2)]
        d_res = sem("d_res")
        d_w = {n: sem(f"d_w_{n}") for n, _, _ in NAMES}
        d_wf, d_cols, d_rows = sem("d_wf"), sem("d_cols"), sem("d_rows")
        g_const = sem("g_const")
        g_xrstd, g_hlo, g_zlo, g_x1stat, g_chain = (sem(n) for n in ("g_xrstd", "g_hlo", "g_zlo", "g_x1stat", "g_chain"))
        a_whi = sem("a_whi")
        a_xnhi, a_tap, a_xs, a_xshi = (sem(n) for n in ("a_xnhi", "a_tap", "a_xs", "a_xshi"))
        a_exp, a_ln, a_decay, a_hhi = (sem(n) for n in ("a_exp", "a_ln", "a_decay", "a_hhi"))
        a_s, a_shi, a_gate, a_zhi, a_x1n = (sem(n) for n in ("a_s", "a_shi", "a_gate", "a_zhi", "a_x1n"))
        p_xT, p_w1, p_prod, p_ssm, p_gate, p_mix, p_small = (
            sem(n) for n in ("p_xT", "p_w1", "p_prod", "p_ssm", "p_gate", "p_mix", "p_small"))
        v_init, v_wlo = sem("v_init"), sem("v_wlo")
        v_xstat, v_xn, v_xnlo, v_tap, v_conv, v_xslo = (
            sem(n) for n in ("v_xstat", "v_xn", "v_xnlo", "v_tap", "v_conv", "v_xslo"))
        v_cap, v_delta, v_da, v_cum, v_gated, v_h = (
            sem(n) for n in ("v_cap", "v_delta", "v_da", "v_cum", "v_gated", "v_h"))
        v_slo, v_z, v_x1, v_x1st, v_ext, v_chain = (
            sem(n) for n in ("v_slo", "v_z", "v_x1", "v_x1st", "v_ext", "v_chain"))
        held = sem("held")
        v_chain_w, v_chain_g = sem("v_chain_w"), sem("v_chain_g")
        g_chain_0, g_x1a, g_x1b = sem("g_chain_0"), sem("g_x1a"), sem("g_x1b")
        q_norm, q_T, q_evac, q_clip, q_hi_s, q_lo0, q_lo1, q_y, q_fin = (
            sem(n) for n in ("q_norm", "q_T", "q_evac", "q_clip", "q_hi", "q_lo0", "q_lo1", "q_y", "q_fin"))

        def col(name, m):
            return cols[:, col_at[name] + m:col_at[name] + m + 1]

        def wait(eng, s, value):
            if isinstance(value, int) and value <= 0:
                return
            eng.wait_ge(s, value)

        def nth(n, r, slots):
            return 16 // slots * (n - r) + 16

        def hold(eng):
            eng.sem_inc(held, 1)

        def run_steps(eng, step):
            for t in range(4):
                step(t, t % 2, t < B, 0 <= t - 1 < B, t >= 2, t >= 3)
            with eng.Fori(2, B // 2 - 1) as i:
                for u in range(2):
                    step(2 * i + u, u, True, True, True, True)
            for t in range(B - 2, B + 2):
                step(t, t % 2, t < B, t - 1 < B, True, True)

        block = ctx.enter_context(nc.Block())

        @block.sync
        def _(sp):
            def load_x(n, r):
                wait(sp, v_xn, n - 1)
                sp.dma_start(x_in[:, r, :, :], x_v[bass.ds(n, 1)].rearrange("o p t d -> (o p) t d")).then_inc(d_x[r], 16)

            sp.dma_start(x_in[:, 0, :, :], x_v[0]).then_inc(d_x[0], 16)
            w_dram = {"w1": w1T, "dl": dlT, "A": AT, "B": BT, "C": CT, "D": DT, "w2": w2T, "w3": w3T}
            for name, _, _ in NAMES:
                sp.dma_start(raw[name], w_dram[name].rearrange("(k p) o -> p k o", p=P)).then_inc(d_w[name], 16)
                if name == "w1":
                    sp.dma_start(cols[:, :], columns).then_inc(d_cols, 16)
                    sp.dma_start(x_in[:, 1, :, :], x_v[1]).then_inc(d_x[1], 16)
            sp.dma_start(raw_ffn[:, :, 0:D], ffn_w.rearrange("(k p) o -> p k o", p=P)).then_inc(d_wf, 16)
            sp.dma_start(g_row[:, :], gamma_row.partition_broadcast(P)).then_inc(d_rows, 16)
            sp.dma_start(b_row[:, :], beta_row.partition_broadcast(P)).then_inc(d_rows, 16)

            def step(t, u, front, hidden, back, back_before):
                if front and not (isinstance(t, int) and t + 2 >= B):
                    load_x(t + 2, u)
                if back:
                    n = t - 2
                    wait(sp, v_x1, 2 * n)
                    sp.dma_start(x_res[:, :, :], x_v[bass.ds(n, 1)].rearrange("o p t d -> (o p) t d")).then_inc(d_res, 16)
                    sp.wait_ge(g_x1stat, n + 1)
                    sp.dma_start(scratch[bass.ds(n, 1)].rearrange("o p f -> (o p) f"),
                                 x1[:, u, :, :].rearrange("p t d -> p (t d)")).then_inc(d_store[u], 16)

            for t in range(4):
                step(t, t % 2, True, True, t >= 2, t >= 3)
            with sp.Fori(2, B // 2 - 1) as i:
                for u in range(2):
                    step(2 * i + u, u, True, True, True, True)
            for t in range(B - 2, B):
                step(t, t % 2, True, True, True, True)
            for t in range(B, B + 2):
                step(t, t % 2, False, True, True, True)

            def load_x1(n, r):
                wait(sp, q_fin, 2 * (n - R1) + 2)
                sp.dma_start(x1_in[:, r, :, :].rearrange("p t d -> p (t d)"),
                             scratch[bass.ds(n, 1)].rearrange("o p f -> (o p) f")).then_inc(d_x1[r], 16)

            def store(n, r):
                sp.wait_ge(q_fin, 2 * n + 2)
                sp.dma_start(out_v[bass.ds(n, 1)].rearrange("o p t d -> (o p) t d"), y_out[r][:, :, :]).then_inc(d_out[r], 16)

            sp.wait_ge(g_hlo, HD * B)
            sp.wait_ge(a_hhi, HD * B)
            for r in range(2):
                sp.wait_ge(d_store[r], nth(B - 2 + r, r, 2))
            for n in range(R1):
                load_x1(n, n)
            for n in range(R1, 2 * R1):
                store(n - R1, n % 2)
                load_x1(n, n % R1)
            with sp.Fori(2, B // 4) as i:
                for r in range(4):
                    store(4 * i + (r - R1), r % 2)
                    load_x1(4 * i + r, r)
            for n in range(B - R1, B):
                store(n, n % 2)
            for r in range(2):
                sp.wait_ge(d_out[r], nth(B - 2 + r, r, 2))

        @block.tensor
        def _(pe):
            def product(bank, name, m, x_hi, x_lo, first=True, last=True):
                kt = w_hi[name].shape[1]
                for k in range(kt):
                    hi = w_hi[name][:, k, m * P:(m + 1) * P]
                    lo = w_lo[name][:, k, m * P:(m + 1) * P]
                    pe.matmul(bank, hi, x_hi[:, k, :], start=(first and k == 0), stop=False)
                    pe.matmul(bank, hi, x_lo[:, k, :], start=False, stop=False)
                    done = pe.matmul(bank, lo, x_hi[:, k, :], start=False, stop=(last and k == kt - 1))
                return done

            def hidden_products(n, u, j, which):
                q = HD * n + j
                xh, xl = xs_hi[:, 1 - u], xs_lo[:, 1 - u]
                for k in which:
                    if k == 0:
                        if j == 0:
                            pe.wait_ge(v_xslo, CD * n + CD)
                        wait(pe, v_delta, q - 1)
                    elif k == 1:
                        wait(pe, v_da, q - 1)
                    else:
                        wait(pe, v_gated, q - 1)
                    product(hb[:, 3 * (j % 2) + k, :], ("dl", "A", "B")[k], j, xh, xl).then_inc(p_prod, 1)

            def step(t, u, front, hidden, back, back_before):
                first = isinstance(t, int)
                if hidden:
                    if first and t == 1:
                        pe.wait_ge(v_wlo, 4)
                    hidden_products(t - 1, u, 0, (0, 1, 2))
                if front:
                    pe.wait_ge(v_xn, t + 1)
                    if first and t == 0:
                        pe.wait_ge(g_const, 1)
                    if back_before:
                        pe.wait_ge(v_x1, 2 * (t - 2))
                    else:
                        wait(pe, v_conv, CD * t)
                    for c in range(CD):
                        for i in range(TT):
                            done = pe.transpose(mb[:, c, i * P:(i + 1) * P], xn[:, i, c * P:(c + 1) * P], ident[:, :])
                        done.then_inc(p_xT, 1)
                if hidden:
                    hidden_products(t - 1, u, 1, (0, 1, 2))
                if back:
                    n = t - 2
                    if first and t == 2:
                        pe.wait_ge(v_wlo, len(NAMES))
                        pe.wait_ge(v_init, 1)
                    pe.wait_ge(a_hhi, HD * n + HD)
                    pe.wait_ge(g_hlo, HD * n + HD)
                    if front:
                        pe.wait_ge(v_xnlo, CD * t + CD)
                    else:
                        pe.wait_ge(v_x1, 2 * n)
                    for m in range(CD):
                        product(mb[:, m, :], "D", m, xs_hi[:, u], xs_lo[:, u], last=False)
                        product(mb[:, m, :], "C", m, h_hi[:, u], h_lo[:, u], first=False).then_inc(p_ssm, 1)
                if hidden:
                    hidden_products(t - 1, u, 2, (0, 1))
                if back:
                    pe.wait_ge(v_slo, CD * n + CD)
                    for m in range(CD):
                        product(mb[:, m, :], "w2", m, s_hi, s_lo).then_inc(p_gate, 1)
                if hidden:
                    hidden_products(t - 1, u, 2, (2,))
                    hidden_products(t - 1, u, 3, (0,))
                if front:
                    if first and t == 0:
                        pe.wait_ge(v_wlo, 1)
                    pe.wait_ge(v_xnlo, CD * t + CD)
                    for m in range(CD):
                        if back:
                            pe.wait_ge(a_gate, CD * (t - 2) + m + 1)
                        product(mb[:, m, :], "w1", m, xn_hi, xn_lo).then_inc(p_w1, 1)
                if hidden:
                    hidden_products(t - 1, u, 3, (1, 2))
                if back:
                    pe.wait_ge(a_zhi, CD * n + CD)
                    pe.wait_ge(g_zlo, CD * n + CD)
                    for i in range(TT):
                        if front and i % 2 == 0:
                            pe.wait_ge(v_conv, CD * t + i // 2 + 1)
                        acc = mb[:, i // 2, (i % 2) * D:(i % 2 + 1) * D]
                        tok = slice(i * P, (i + 1) * P)
                        for k in range(CD):
                            pe.matmul(acc, z_hi[:, k, tok], w_hi["w3"][:, k, :], start=(k == 0), stop=False)
                            pe.matmul(acc, z_hi[:, k, tok], w_lo["w3"][:, k, :], start=False, stop=False)
                            pe.matmul(acc, z_lo[:, k, tok], w_hi["w3"][:, k, :], start=False, stop=(k == CD - 1))
                        for k in range(CD):
                            part = mb[:, i // 2, (i % 2) * D + k * P:(i % 2) * D + (k + 1) * P]
                            pe.matmul(part, s_hi[:, k, tok], ident_r[:, :], start=False, stop=True, skip_group_check=True)
                            done = pe.matmul(part, s_lo[:, k, tok], ident_r[:, :], start=False, stop=True,
                                             skip_group_check=True)
                        if i % 2 == 1:
                            done.then_inc(p_mix, 1)

            pe.wait_ge(v_init, 2)
            pe.wait_ge(g_const, 1)
            pe.matmul(hb[:, 5, 0:1], ones[:, :], scal[:, 0:1], start=True, stop=True).then_inc(p_small, 1)
            pe.wait_ge(v_init, 3)

            run_steps(pe, step)

            pe.wait_ge(v_chain, 1)
            pe.transpose(hb[0:1, 0, 0:P], scal[:, 1:2], ident[:, :]).then_inc(p_small, 1)
            pe.wait_ge(v_chain, 2)
            pe.matmul(hb[:, 1, 0:1], ones[0:1, :], scal[0:1, 2:3], start=True, stop=True).then_inc(p_small, 1)

            def y_bank(r, half):
                return hb[:, 4 + half, :] if r == 0 else mb[:, half, :]

            def transposes(n, r):
                pe.wait_ge(q_norm, n + 1)
                wait(pe, q_evac, CD * (n - 1))
                for c in range(CD):
                    for i in range(TT):
                        done = pe.transpose(hb[:, 2 * r + c, i * P:(i + 1) * P], xn2[:, r, i, c * P:(c + 1) * P], ident[:, :])
                    done.then_inc(q_T, 1)

            def projection(n, r):
                pe.wait_ge(q_lo0, n + 1)
                pe.wait_ge(q_lo1, n + 1)
                wait(pe, q_fin, 2 * (n - 1))
                for i in range(TT):
                    acc = y_bank(r, i // 2)[:, (i % 2) * D:(i % 2 + 1) * D]
                    tok = slice(i * P, (i + 1) * P)
                    for k in range(CD):
                        pe.matmul(acc, q_hi[:, r, k, tok], wq[:, k, :], start=(k == 0), stop=False)
                        done = pe.matmul(acc, q_lo[:, r, k, tok], wq[:, k, :], start=False, stop=(k == CD - 1))
                    if i % 2 == 1:
                        done.then_inc(q_y, 1)

            pe.wait_ge(v_chain, 3)
            transposes(0, 0)
            for n in range(2):
                transposes(n + 1, 1 - n)
                projection(n, n)
            with pe.Fori(1, B // 2 - 1) as i:
                for u in range(2):
                    transposes(2 * i + u + 1, 1 - u)
                    projection(2 * i + u, u)
            transposes(B - 1, 1)
            projection(B - 2, 0)
            projection(B - 1, 1)

        @block.scalar
        def _(act):
            act.preload_act_table_set(EXP_LN_TABLE)
            for name, _, _ in NAMES:
                act.wait_ge(d_w[name], 16)
                act.activation(w_hi[name][:, :, :], raw[name], ACT.Copy).then_inc(a_whi, 1)

            def hidden_in(n, j):
                q = HD * n + j
                act.wait_ge(p_prod, 3 * q + 1)
                act.activation(softp[:, j % 2, :], hb[:, 3 * (j % 2), :], ACT.Exp, bias=col("dl_b", j)).then_inc(a_exp, 1)
                act.wait_ge(v_cap, q + 1)
                act.activation(softp[:, j % 2, :], softp[:, j % 2, :], ACT.Ln, bias=1.0).then_inc(a_ln, 1)

            def decay(n, j):
                act.wait_ge(v_cum, HD * n + j + 1)
                act.activation(cumul[:, j % 2, :], cumul[:, j % 2, :], ACT.Exp, scale=-1.0).then_inc(a_decay, 1)

            def hidden_hi(n, r, j):
                act.wait_ge(v_h, HD * n + j + 1)
                if j == 0:
                    wait(act, p_ssm, CD * (n - 1))
                act.activation(h_hi[:, r, j, :], hsum[:, j % 2, :], ACT.Copy).then_inc(a_hhi, 1)

            def step(t, u, front, hidden, back, back_before):
                first = isinstance(t, int)
                if hidden:
                    if first and t == 1:
                        act.wait_ge(v_wlo, len(NAMES))
                    hidden_in(t - 1, 0)
                if back:
                    hidden_hi(t - 2, u, HD - 1)
                if front:
                    for c in range(CD):
                        act.wait_ge(p_xT, CD * t + c + 1)
                        wait(act, p_w1, CD * t)
                        act.activation(xn_hi[:, c, :], mb[:, c, :], ACT.Copy).then_inc(a_xnhi, 1)
                if hidden:
                    decay(t - 1, 0)
                if back_before:
                    n = t - 3
                    act.wait_ge(g_x1stat, n + 1)
                    if first and t == 3:
                        act.wait_ge(v_wlo, len(NAMES))
                    wait(act, v_ext, n)
                    for i in range(TT):
                        done = act.activation(x1n[:, i, :], x1[:, 1 - u, i, 0:D], ACT.Identity,
                                              scale=x1[:, 1 - u, i, D:D + 1], bias=x1[:, 1 - u, i, D + 1:D + 2])
                    done.then_inc(a_x1n, 1)
                if hidden:
                    hidden_in(t - 1, 1)
                    hidden_hi(t - 1, 1 - u, 0)
                    decay(t - 1, 1)
                if back:
                    n = t - 2
                    for m in range(CD):
                        act.wait_ge(p_ssm, CD * n + m + 1)
                        wait(act, p_mix, 2 * n)
                        if first and t == 2:
                            act.wait_ge(v_init, 4)
                        act.activation(s_buf[:, m, :], mb[:, m, :], ACT.Identity, bias=cd_b[:, m:m + 1]).then_inc(a_s, 1)
                        act.activation(s_hi[:, m, :], mb[:, m, :], ACT.Identity, bias=cd_b[:, m:m + 1]).then_inc(a_shi, 1)
                if hidden:
                    hidden_in(t - 1, 2)
                    hidden_hi(t - 1, 1 - u, 1)
                    decay(t - 1, 2)
                if front or back:
                    act.preload_act_table_set(SILU_TABLE)
                if back:
                    for m in range(CD):
                        act.wait_ge(p_gate, CD * n + m + 1)
                        act.activation(gate[:, m, :], mb[:, m, :], ACT.Silu).then_inc(a_gate, 1)
                if front:
                    for c in range(CD):
                        act.wait_ge(p_w1, CD * t + c + 1)
                        wait(act, v_xslo, CD * t)
                        if first and t == 0:
                            act.wait_ge(d_cols, 16)
                        act.activation(xs[:, c, :], mb[:, c, :], ACT.Identity, scale=col("conv_w1", c),
                                       bias=col("conv_b", c)).then_inc(a_tap, 1)
                if back:
                    for m in range(CD):
                        act.wait_ge(v_z, CD * n + m + 1)
                        act.activation(z_hi[:, m, :], z_buf[:, m, :], ACT.Copy).then_inc(a_zhi, 1)
                if front:
                    for c in range(CD):
                        act.wait_ge(v_conv, CD * t + c + 1)
                        act.activation(xs[:, c, :], xs[:, c, :], ACT.Silu).then_inc(a_xs, 1)
                        act.wait_ge(a_xs, CD * t + c + 1)
                        wait(act, p_ssm, CD * (t - 1))
                        act.activation(xs_hi[:, u, c, :], xs[:, c, :], ACT.Copy).then_inc(a_xshi, 1)
                if front or back:
                    act.preload_act_table_set(EXP_LN_TABLE)
                if hidden:
                    hidden_in(t - 1, 3)
                    hidden_hi(t - 1, 1 - u, 2)
                    decay(t - 1, 3)

            run_steps(act, step)

            act.wait_ge(g_x1stat, B)
            act.wait_ge(v_ext, B - 1)
            for i in range(TT):
                done = act.activation(x1n[:, i, :], x1[:, 1, i, 0:D], ACT.Identity,
                                      scale=x1[:, 1, i, D:D + 1], bias=x1[:, 1, i, D + 1:D + 2])
            done.then_inc(a_x1n, 1)

            act.wait_ge(v_chain, 4)

            def evacuate(n, r):
                for c in range(CD):
                    act.wait_ge(q_T, CD * n + c + 1)
                    wait(act, q_lo1, n - 1)
                    wait(act, q_lo0, n - 1)
                    act.activation(xc[r][:, c, :], hb[:, 2 * r + c, :], ACT.Identity, scale=scal[:, 6 + c:7 + c],
                                   bias=scal[:, 8 + c:9 + c]).then_inc(q_evac, 1)

            def split_hi(n, r):
                wait(act, q_y, 2 * (n - 1))
                for c in range(CD):
                    act.wait_ge(q_clip, CD * n + c + 1)
                    act.activation(q_hi[:, r, c, :], xc[r][:, c, :], ACT.Copy).then_inc(q_hi_s, 1)

            evacuate(0, 0)
            for n in range(2):
                split_hi(n, n)
                evacuate(n + 1, 1 - n)
            with act.Fori(1, B // 2 - 1) as i:
                for u in range(2):
                    split_hi(2 * i + u, u)
                    evacuate(2 * i + u + 1, 1 - u)
            split_hi(B - 2, 0)
            evacuate(B - 1, 1)
            split_hi(B - 1, 1)

        @block.vector
        def _(dve):
            def raw_f32(ap):
                return ap.bitcast(F32)

            def x_statistics(n, r):
                dve.wait_ge(d_x[r], nth(n, r, 2))
                wait(dve, v_xn, n)
                for i in range(TT):
                    done = dve.bn_stats(x_stat[:, i, :], x_in[:, r, i, :])
                done.then_inc(v_xstat, 1)
                dve.wait_ge(v_xstat, 2 * n + 1)
                hold(dve)
                for i in range(TT):
                    done = dve.bn_aggr(x_mv[:, i, :], x_stat[:, i, :])
                done.then_inc(v_xstat, 1)

            def x_normalise(n, r):
                dve.wait_ge(g_xrstd, n + 1)
                wait(dve, p_xT, CD * n)
                for i in range(TT):
                    done = dve.tensor_scalar(xn[:, i, :], x_in[:, r, i, :], x_mv[:, i, 0:1], x_rstd[:, i:i + 1],
                                             ALU.subtract, ALU.mult)
                done.then_inc(v_xn, 1)

            x_statistics(0, 0)

            def split_weight(k, name):
                dve.wait_ge(a_whi, k + 1)
                dve.tensor_tensor(w_lo[name][:, :, :], raw[name], raw_f32(w_hi[name][:, :, :]), ALU.subtract).then_inc(v_wlo, 1)

            split_weight(0, "w1")
            x_normalise(0, 0)
            for k, (name, _, _) in enumerate(NAMES[1:4]):
                split_weight(k + 1, name)
            dve.wait_ge(g_const, 1)
            dve.tensor_copy(ident_r[:, :], ident[:, :]).then_inc(v_init, 1)
            dve.wait_ge(d_wf, 16)
            dve.tensor_reduce(scal[:, 0:1], raw_ffn[:, :, 0:D], AX.XY, ALU.add, apply_absolute_value=True).then_inc(v_init, 1)
            dve.wait_ge(p_small, 1)
            dve.tensor_scalar(scal[:, 3:4], hb[:, 5, 0:1], 1.0 / (D * D), None, ALU.mult).then_inc(v_chain_w, 1)
            dve.wait_ge(v_chain_w, 1)
            dve.tensor_scalar(scal[:, 4:5], scal[:, 3:4], Q_EPS, None, ALU.add).then_inc(v_chain_w, 1)
            dve.wait_ge(v_chain_w, 2)
            dve.reciprocal(scal[:, 5:6], scal[:, 4:5]).then_inc(v_chain_w, 1)
            dve.wait_ge(v_chain_w, 3)
            wf = raw_ffn[:, :, 0:D]
            dve.tensor_scalar(wf, wf, scal[:, 5:6], ROUND_MAGIC, ALU.mult, ALU.add).then_inc(v_chain_w, 1)
            dve.wait_ge(v_chain_w, 4)
            dve.tensor_scalar(wf, wf, ROUND_MAGIC, 1.0, ALU.subtract, ALU.min).then_inc(v_chain_w, 1)
            dve.wait_ge(v_chain_w, 5)
            dve.tensor_scalar(wq[:, :, :], wf, -1.0, None, ALU.max).then_inc(v_init, 1)
            for k, (name, _, _) in enumerate(NAMES[4:]):
                split_weight(k + 4, name)
            dve.wait_ge(d_cols, 16)
            dve.tensor_tensor(cd_b[:, :], cols[:, col_at["C_b"]:col_at["C_b"] + CD],
                              cols[:, col_at["D_b"]:col_at["D_b"] + CD], ALU.add).then_inc(v_init, 1)
            dve.memset(hi_run[:, :, :], -BIG)
            dve.memset(lo_run[:, :, :], BIG).then_inc(v_init, 1)

            def cap(n, j):
                q = HD * n + j
                dve.wait_ge(a_exp, q + 1)
                dve.tensor_scalar(softp[:, j % 2, :], softp[:, j % 2, :], EXP_CAP, None, ALU.min).then_inc(v_cap, 1)

            def decay_exponent(n, j):
                q = HD * n + j
                dve.wait_ge(a_ln, q + 1)
                dve.scalar_tensor_tensor(out=delta[:, j % 2, :], in0=hb[:, 3 * (j % 2), :], scalar=col("dl_b", j),
                                         in1=softp[:, j % 2, :], op0=ALU.add, op1=ALU.max).then_inc(v_delta, 1)
                dve.wait_ge(p_prod, 3 * q + 2)
                dve.wait_ge(v_delta, q + 1)
                dve.scalar_tensor_tensor(out=delta[:, j % 2, :], in0=hb[:, 3 * (j % 2) + 1, :], scalar=col("A_b", j),
                                         in1=delta[:, j % 2, :], op0=ALU.add, op1=ALU.mult).then_inc(v_da, 1)
                dve.wait_ge(v_da, q + 1)
                dve.tensor_tensor_scan(out=cumul[:, j % 2, :], data0=delta[:, j % 2, :], data1=delta[:, j % 2, :],
                                       initial=0.0, op0=ALU.add, op1=ALU.bypass).then_inc(v_cum, 1)

            def hidden_state(n, j):
                q = HD * n + j
                dve.wait_ge(p_prod, 3 * q + 3)
                dve.wait_ge(a_decay, q + 1)
                wait(dve, a_hhi, q - 1)
                wait(dve, g_hlo, q - 1)
                dve.scalar_tensor_tensor(out=gated[:, j % 2, :], in0=hb[:, 3 * (j % 2) + 2, :], scalar=col("B_b", j),
                                         in1=cumul[:, j % 2, :], op0=ALU.add, op1=ALU.mult).then_inc(v_gated, 1)
                dve.wait_ge(v_gated, q + 1)
                dve.tensor_tensor_scan(out=hsum[:, j % 2, :], data0=gated[:, j % 2, :], data1=gated[:, j % 2, :],
                                       initial=0.0, op0=ALU.add, op1=ALU.bypass).then_inc(v_h, 1)

            def extrema(n):
                dve.wait_ge(a_x1n, n + 1)
                if isinstance(n, int) and n == 0:
                    dve.wait_ge(v_init, 5)
                else:
                    dve.wait_ge(v_ext, n)
                dve.tensor_tensor(hi_run[:, :, :], hi_run[:, :, :], x1n[:, :, :], ALU.max)
                dve.tensor_tensor(lo_run[:, :, :], lo_run[:, :, :], x1n[:, :, :], ALU.min).then_inc(v_ext, 1)

            def step(t, u, front, hidden, back, back_before):
                last = isinstance(t, int) and t + 1 >= B
                if hidden:
                    cap(t - 1, 0)
                if back:
                    hidden_state(t - 2, HD - 1)
                if hidden:
                    decay_exponent(t - 1, 0)
                if front:
                    for c in range(CD):
                        dve.wait_ge(a_xnhi, CD * t + c + 1)
                        dve.tensor_tensor(xn_lo[:, c, :], mb[:, c, :], raw_f32(xn_hi[:, c, :]), ALU.subtract).then_inc(v_xnlo, 1)
                if hidden:
                    cap(t - 1, 1)
                    hidden_state(t - 1, 0)
                    decay_exponent(t - 1, 1)
                if back_before:
                    extrema(t - 3)
                if back:
                    n = t - 2
                    for m in range(CD):
                        dve.wait_ge(a_shi, CD * n + m + 1)
                        dve.tensor_tensor(s_lo[:, m, :], s_buf[:, m, :], raw_f32(s_hi[:, m, :]), ALU.subtract).then_inc(v_slo, 1)
                if hidden:
                    cap(t - 1, 2)
                    hidden_state(t - 1, 1)
                    decay_exponent(t - 1, 2)
                if front and not last:
                    x_statistics(t + 1, 1 - u)
                if back:
                    for m in range(CD):
                        dve.wait_ge(a_gate, CD * n + m + 1)
                        wait(dve, g_zlo, CD * n)
                        wait(dve, a_zhi, CD * n)
                        dve.tensor_tensor(z_buf[:, m, :], gate[:, m, :], s_buf[:, m, :], ALU.mult).then_inc(v_z, 1)
                if front:
                    for c in range(CD):
                        dve.wait_ge(a_tap, CD * t + c + 1)
                        dve.scalar_tensor_tensor(out=xs[:, c, 1:L], in0=mb[:, c, 0:L - 1], scalar=col("conv_w0", c),
                                                 in1=xs[:, c, 1:L], op0=ALU.mult, op1=ALU.add).then_inc(v_tap, 1)
                        dve.wait_ge(v_tap, CD * t + c + 1)
                        dve.scalar_tensor_tensor(out=xs[:, c, 0:L - 1], in0=mb[:, c, 1:L], scalar=col("conv_w2", c),
                                                 in1=xs[:, c, 0:L - 1], op0=ALU.mult, op1=ALU.add).then_inc(v_conv, 1)
                    for c in range(CD):
                        dve.wait_ge(a_xshi, CD * t + c + 1)
                        dve.tensor_tensor(xs_lo[:, u, c, :], xs[:, c, :], raw_f32(xs_hi[:, u, c, :]),
                                          ALU.subtract).then_inc(v_xslo, 1)
                if hidden:
                    cap(t - 1, 3)
                    hidden_state(t - 1, 2)
                    decay_exponent(t - 1, 3)
                if front and not last:
                    x_normalise(t + 1, 1 - u)
                if back:
                    dve.wait_ge(d_res, 16 * n + 16)
                    wait(dve, d_store[u], nth(n - 2, u, 2))
                    wait(dve, a_x1n, n - 1)
                    for half in range(2):
                        dve.wait_ge(p_mix, 2 * n + half + 1)
                        dve.tensor_tensor(x1[:, u, 2 * half:2 * half + 2, 0:D], x_res[:, 2 * half:2 * half + 2, :],
                                          mb[:, half, :].rearrange("p (t d) -> p t d", t=2), ALU.add).then_inc(v_x1, 1)
                    wait(dve, g_x1stat, n)
                    for i in range(TT):
                        if i % 2 == 0:
                            dve.wait_ge(v_x1, 2 * n + i // 2 + 1)
                        done = dve.bn_stats(x1_stat[:, i, :], x1[:, u, i, 0:D])
                    done.then_inc(v_x1st, 1)
                    dve.wait_ge(v_x1st, 2 * n + 1)
                    hold(dve)
                    for i in range(TT):
                        done = dve.bn_aggr(x1_mv[:, i, :], x1_stat[:, i, :])
                    done.then_inc(v_x1st, 1)

            run_steps(dve, step)
            extrema(B - 1)

            count = [0]

            def chained(ins):
                count[0] += 1
                ins.then_inc(v_chain_g, 1)
                dve.wait_ge(v_chain_g, count[0])

            dve.wait_ge(v_ext, B)
            dve.wait_ge(d_rows, 32)
            ext = [x_in[:, 0, 0, :], x_in[:, 0, 1, :]]
            chained(dve.tensor_reduce(ext[0], hi_run[:, :, :].rearrange("p t d -> p d t"), AX.X, ALU.max))
            chained(dve.tensor_reduce(ext[1], lo_run[:, :, :].rearrange("p t d -> p d t"), AX.X, ALU.min))
            for e in ext:
                chained(dve.tensor_tensor(e, e, g_row[:, :], ALU.mult))
                chained(dve.tensor_tensor(e, e, b_row[:, :], ALU.add))
            dve.tensor_reduce(scal[:, 1:2], x_in[:, 0, 0:2, :], AX.XY, ALU.max, apply_absolute_value=True).then_inc(v_chain, 1)
            dve.wait_ge(p_small, 2)
            dve.reduce_max(scal[0:1, 2:3], hb[0:1, 0, 0:P], axis=AX.X).then_inc(v_chain, 1)
            dve.wait_ge(p_small, 3)
            dve.tensor_copy(scal[:, 10:11], hb[:, 1, 0:1]).then_inc(v_chain, 1)
            dve.wait_ge(v_chain, 3)
            chained(dve.reciprocal(scal[:, 11:12], scal[:, 10:11]))
            chained(dve.tensor_scalar(scal[:, 12:13], scal[:, 11:12], QB, None, ALU.mult))
            chained(dve.tensor_scalar(scal[:, 13:14], scal[:, 10:11], scal[:, 3:4], 1.0 / QB, ALU.mult, ALU.mult))
            chained(dve.tensor_scalar(scal[:, 6:8], cols[:, col_at["ln_gamma"]:col_at["ln_gamma"] + CD],
                                      scal[:, 12:13], None, ALU.mult))
            dve.tensor_scalar(scal[:, 8:10], cols[:, col_at["ln_beta"]:col_at["ln_beta"] + CD],
                              scal[:, 12:13], None, ALU.mult).then_inc(v_chain, 1)

            def normalise(n, r, r4):
                dve.wait_ge(d_x1[r4], nth(n, r4, 4))
                wait(dve, q_T, CD * (n - 1))
                for i in range(TT):
                    done = dve.tensor_scalar(xn2[:, r, i, :], x1_in[:, r4, i, 0:D], x1_in[:, r4, i, D:D + 1],
                                             x1_in[:, r4, i, D + 1:D + 2], ALU.mult, ALU.add)
                done.then_inc(q_norm, 1)

            def clip(n, r):
                for c in range(CD):
                    dve.wait_ge(q_evac, CD * n + c + 1)
                    dve.tensor_scalar(xc[r][:, c, :], xc[r][:, c, :], CLIP, -CLIP, ALU.min, ALU.max).then_inc(q_clip, 1)

            def split_lo(n, r):
                dve.wait_ge(q_hi_s, CD * n + 2)
                dve.tensor_tensor(q_lo[:, r, 1, :], xc[r][:, 1, :], raw_f32(q_hi[:, r, 1, :]), ALU.subtract).then_inc(q_lo1, 1)

            def finish(n, r, r4):
                wait(dve, d_out[r], nth(n - 2, r, 2))
                for half in range(2):
                    dve.wait_ge(q_y, 2 * n + half + 1)
                    src = hb[:, 4 + half, :] if r == 0 else mb[:, half, :]
                    dve.scalar_tensor_tensor(out=y_out[r][:, 2 * half:2 * half + 2, :], in0=src.rearrange("p (t d) -> p t d", t=2),
                                             scalar=scal[:, 13:14], in1=x1_in[:, r4, 2 * half:2 * half + 2, 0:D],
                                             op0=ALU.mult, op1=ALU.add).then_inc(q_fin, 1)

            dve.wait_ge(v_chain, 4)
            normalise(0, 0, 0)

            def step2(t, u, u4, before, after):
                if after:
                    normalise(t + 1, 1 - u, (u4 + 1) % 4)
                clip(t, u)
                if before:
                    finish(t - 1, 1 - u, (u4 + 3) % 4)
                split_lo(t, u)

            for t in range(4):
                step2(t, t % 2, t, t > 0, True)
            with dve.Fori(1, B // 4 - 1) as i:
                for u4 in range(4):
                    step2(4 * i + u4, u4 % 2, u4, True, True)
            for t in range(B - 4, B):
                step2(t, t % 2, t % 4, True, t + 1 < B)
            finish(B - 1, 1, 3)

        @block.gpsimd
        def _(pool):
            chain = [0]

            def chained(ins):
                chain[0] += 1
                ins.then_inc(g_chain_0, 1)
                pool.wait_ge(g_chain_0, chain[0])

            chained(pool.memset(ident[:, :], 0.0))
            chained(pool.memset(ones[:, :], 1.0))
            chained(pool.memset(neg_half[:, :], -0.5))
            pool.affine_select(out=ident[:, :], in_=ident[:, :], compare_op=ALU.not_equal, fill=1.0, base=0,
                               pattern=[[-1, P]], channel_multiplier=1).then_inc(g_const, 1)

            def x_rstd_of(n):
                pool.wait_ge(v_xstat, 2 * n + 2)
                wait(pool, v_xn, n)
                hold(pool)
                pool.tensor_scalar(x_rstd[:, :], x_mv[:, :, 1], LN_EPS, None, ALU.add).then_inc(g_chain, 1)
                pool.wait_ge(g_chain, n + 1)
                pool.tensor_tensor(x_rstd[:, :], x_rstd[:, :], neg_half[:, :], ALU.pow).then_inc(g_xrstd, 1)

            def x1_rstd_of(n, r):
                pool.wait_ge(v_x1st, 2 * n + 2)
                hold(pool)
                pool.tensor_scalar(x1_tmp[:, 0, :], x1_mv[:, :, 1], 1.0 + FFN_LN_EPS, LN_EPS * FFN_LN_EPS,
                                   ALU.mult, ALU.add).then_inc(g_x1a, 1)
                pool.tensor_scalar(x1_tmp[:, 1, :], x1_mv[:, :, 0], -1.0, 0.0, ALU.mult, ALU.add).then_inc(g_x1a, 1)
                pool.wait_ge(g_x1a, 2 * n + 2)
                wait(pool, d_store[r], nth(n - 2, r, 2))
                wait(pool, a_x1n, n - 1)
                pool.tensor_tensor(x1[:, r, :, D], x1_tmp[:, 0, :], neg_half[:, :], ALU.pow).then_inc(g_x1b, 1)
                pool.wait_ge(g_x1b, n + 1)
                pool.tensor_tensor(x1[:, r, :, D + 1], x1_tmp[:, 1, :], x1[:, r, :, D], ALU.mult).then_inc(g_x1stat, 1)

            def hidden_lo(n, r, j):
                pool.wait_ge(a_hhi, HD * n + j + 1)
                if j == 0:
                    wait(pool, p_ssm, CD * (n - 1))
                pool.tensor_tensor(h_lo[:, r, j, :], hsum[:, j % 2, :], h_hi[:, r, j, :].bitcast(F32),
                                   ALU.subtract).then_inc(g_hlo, 1)

            x_rstd_of(0)

            def step(t, u, front, hidden, back, back_before):
                last = isinstance(t, int) and t + 1 >= B
                n = t - 2
                if back:
                    hidden_lo(n, u, HD - 1)
                if hidden:
                    hidden_lo(t - 1, 1 - u, 0)
                    hidden_lo(t - 1, 1 - u, 1)
                if front and not last:
                    x_rstd_of(t + 1)
                if back:
                    wait(pool, p_mix, 2 * n)
                    for m in range(CD):
                        pool.wait_ge(a_zhi, CD * n + m + 1)
                        pool.tensor_tensor(z_lo[:, m, :], z_buf[:, m, :], z_hi[:, m, :].bitcast(F32),
                                           ALU.subtract).then_inc(g_zlo, 1)
                if hidden:
                    hidden_lo(t - 1, 1 - u, 2)
                if back:
                    x1_rstd_of(n, u)

            run_steps(pool, step)

            def split_lo(n, r):
                pool.wait_ge(q_hi_s, CD * n + 1)
                pool.tensor_tensor(q_lo[:, r, 0, :], xc[r][:, 0, :], q_hi[:, r, 0, :].bitcast(F32),
                                   ALU.subtract).then_inc(q_lo0, 1)

            with pool.Fori(0, B // 2) as i:
                for u in range(2):
                    split_lo(2 * i + u, u)


def kernel(**inputs):
    import concourse.bacc as _bacc
    from concourse.bass_utils import run_bass_kernel_spmd as _run

    a = {k.split("L0_")[1]: np.asarray(v) for k, v in inputs.items()}
    D, H = a["attn_w1"].shape[0], a["attn_A_w"].shape[0]

    def tiles(v):
        return np.ascontiguousarray(v.reshape(-1, P).T)

    conv = a["attn_conv_w"].reshape(D, 3)
    named = {"dl_b": a["attn_dl_b"], "A_b": a["attn_A_b"], "B_b": a["attn_B_b"], "C_b": a["attn_C_b"],
             "D_b": a["attn_D_b"], "conv_b": a["attn_conv_b"], "conv_w0": conv[:, 0], "conv_w1": conv[:, 1],
             "conv_w2": conv[:, 2], "ln_gamma": a["ffn_ln_gamma"], "ln_beta": a["ffn_ln_beta"]}
    where, _ = column_layout(D, H)
    columns = np.concatenate([tiles(named[n]) for n in where], axis=1)
    arrays = {"x": a["attn_x"], "w1T": a["attn_w1"].T, "w2T": a["attn_w2"].T, "w3T": a["attn_w3"].T,
              "dlT": a["attn_dl_w"].T, "AT": a["attn_A_w"].T, "BT": a["attn_B_w"].T, "CT": a["attn_C_w"].T,
              "DT": a["attn_D_w"].T, "ffn_w": a["ffn_weight"], "columns": columns,
              "gamma_row": a["ffn_ln_gamma"], "beta_row": a["ffn_ln_beta"]}
    arrays = {k: np.ascontiguousarray(v) for k, v in arrays.items()}

    nc = _bacc.Bacc("TRN2", target_bir_lowering=False, num_devices=1)
    args = [nc.dram_tensor(k, v.shape, mybir.dt.from_np(v.dtype), kind="ExternalInput").ap() for k, v in arrays.items()]
    out = nc.dram_tensor("out", a["attn_x"].shape, F32, kind="ExternalOutput").ap()
    build(nc, *args, out)
    r = _run(nc, [arrays], core_ids=[0])
    return r.results[0]["out"]
```

```python
from contextlib import ExitStack

import numpy as np

import concourse.bass as bass
from concourse import mybir

P = 128
F32 = mybir.dt.float32
F32R = mybir.dt.float32r
ALU = mybir.AluOpType
ACT = mybir.ActivationFunctionType
AX = mybir.AxisListType

LN_EPS = 1e-5
FFN_LN_EPS = 1e-3
QB = 128.0
Q_EPS = 1e-5
CLIP = float(np.float32(QB - Q_EPS))
ROUND_MAGIC = 1.5 * 2.0**23
EXP_CAP = 2.0**62
BIG = 3.0e38

EXP_LN_TABLE = "natural_log_exp_and_others"
SILU_TABLE = "silu_and_others"


def column_layout(D, H):
    at, where = 0, {}
    for name, n in [("dl_b", H // P), ("A_b", H // P), ("B_b", H // P), ("C_b", D // P), ("D_b", D // P),
                    ("conv_b", D // P), ("conv_w0", D // P), ("conv_w1", D // P), ("conv_w2", D // P),
                    ("ln_gamma", D // P), ("ln_beta", D // P)]:
        where[name] = at
        at += n
    return where, at


def build(nc, x, w1T, w2T, w3T, dlT, AT, BT, CT, DT, ffn_w, columns, gamma_row, beta_row, out):
    B, L, D = x.shape
    H = dlT.shape[1]
    CD = D // P
    HD = H // P
    TT = L // P
    XW = D + 2
    assert (CD, HD, TT) == (2, 4, 4) and L == 512 and B % 4 == 0 and B >= 12
    col_at, n_cols = column_layout(D, H)

    x_v = x.rearrange("b (t p) d -> b p t d", p=P)
    out_v = out.rearrange("b (t p) d -> b p t d", p=P)
    scratch = nc.dram_tensor("x1_scratch", [B, P, TT * XW], F32, kind="Internal").ap()

    with ExitStack() as ctx:
        def sb(name, shape, dt=F32):
            return ctx.enter_context(nc.sbuf_tensor(name, shape, dt))

        def sem(name):
            return ctx.enter_context(nc.semaphore(name))

        NAMES = [("w1", CD, D), ("dl", CD, H), ("A", CD, H), ("B", CD, H), ("C", HD, D), ("D", CD, D), ("w2", CD, D),
                 ("w3", CD, D)]
        w_hi = {n: sb(f"{n}_hi", [P, k, o], F32R) for n, k, o in NAMES}
        w_lo = {n: sb(f"{n}_lo", [P, k, o], F32R) for n, k, o in NAMES}
        wq = sb("wq", [P, CD, D], F32R)
        ident = sb("ident", [P, P])
        ident_r = sb("ident_r", [P, P], F32R)
        ones = sb("ones", [P, P])
        neg_half = sb("neg_half", [P, TT])
        cols = sb("cols", [P, n_cols])
        cd_b = sb("cd_b", [P, CD])
        g_row = sb("g_row", [P, D])
        b_row = sb("b_row", [P, D])
        hi_run = sb("hi_run", [P, TT, D])
        lo_run = sb("lo_run", [P, TT, D])
        scal = sb("scal", [P, 16])

        x_in = sb("x_in", [P, 2, TT, D])
        x_res = sb("x_res", [P, TT, D])
        x_stat = sb("x_stat", [P, TT, 6])
        x_mv = sb("x_mv", [P, TT, 2])
        x_tmp = sb("x_tmp", [P, 2, TT])
        x_norm = sb("x_norm", [P, 2, TT])
        xn = sb("xn", [P, TT, D])
        xn_hi = sb("xn_hi", [P, CD, L], F32R)
        xn_lo = sb("xn_lo", [P, CD, L], F32R)
        xs = sb("xs", [P, CD, L])
        xs_hi = sb("xs_hi", [P, 2, CD, L], F32R)
        xs_lo = sb("xs_lo", [P, 2, CD, L], F32R)
        temps = sb("temps", [P, 10 * L])

        def temp(k):
            return temps[:, k * 2 * L:(k + 1) * 2 * L].rearrange("p (r l) -> p r l", r=2)

        softp, delta, cumul, gated, hsum = temp(0), temp(1), temp(2), temp(3), temp(4)
        h_hi = sb("h_hi", [P, 2, HD, L], F32R)
        h_lo = sb("h_lo", [P, 2, HD, L], F32R)
        s_buf = sb("s_buf", [P, CD, L])
        s_hi = sb("s_hi", [P, CD, L], F32R)
        s_lo = sb("s_lo", [P, CD, L], F32R)
        gate = sb("gate", [P, CD, L])
        z_buf = sb("z_buf", [P, CD, L])
        z_hi = sb("z_hi", [P, CD, L], F32R)
        z_lo = sb("z_lo", [P, CD, L], F32R)
        x1 = sb("x1", [P, 2, TT, XW])
        x1_stat = sb("x1_stat", [P, TT, 6])
        x1_mv = sb("x1_mv", [P, TT, 2])
        x1_tmp = sb("x1_tmp", [P, 2, TT])
        x1n = sb("x1n", [P, TT, D])

        stage_at, raw = 0, {}
        for name, k, o in NAMES:
            if name == "C":
                raw[name] = x1n[:, :, :].rearrange("p t d -> p (t d)").rearrange("p (k o) -> p k o", k=k)
            else:
                raw[name] = temps[:, stage_at:stage_at + k * o].rearrange("p (k o) -> p k o", k=k)
                stage_at += k * o
        assert stage_at <= 10 * L
        raw_ffn = s_buf

        R1 = 4
        x1_in = temps[:, 0:R1 * TT * XW].rearrange("p (r t d) -> p r t d", r=R1, t=TT)
        xn2 = x_in
        xc = [z_buf, gate]
        q_hi, q_lo = xs_hi, xs_lo
        y_out = [xn, x1n]

        hb = ctx.enter_context(nc.psum_tensor("hidden_banks", [P, 6, L], F32))
        mb = ctx.enter_context(nc.psum_tensor("misc_banks", [P, 2, L], F32))

        d_x = [sem(f"d_x{r}") for r in range(2)]
        d_store = [sem(f"d_store{r}") for r in range(2)]
        d_x1 = [sem(f"d_x1_{r}") for r in range(4)]
        d_out = [sem(f"d_out{r}") for r in range(2)]
        d_res = sem("d_res")
        d_w = {n: sem(f"d_w_{n}") for n, _, _ in NAMES}
        d_wf, d_cols, d_rows = sem("d_wf"), sem("d_cols"), sem("d_rows")
        g_const = sem("g_const")
        g_xnorm, g_hlo, g_zlo, g_x1stat = (sem(n) for n in ("g_xnorm", "g_hlo", "g_zlo", "g_x1stat"))
        a_whi = sem("a_whi")
        a_xn, a_xnhi, a_tap, a_xs, a_xshi = (sem(n) for n in ("a_xn", "a_xnhi", "a_tap", "a_xs", "a_xshi"))
        a_exp, a_ln, a_decay, a_hhi = (sem(n) for n in ("a_exp", "a_ln", "a_decay", "a_hhi"))
        a_s, a_shi, a_gate, a_zhi, a_x1n = (sem(n) for n in ("a_s", "a_shi", "a_gate", "a_zhi", "a_x1n"))
        p_xT, p_w1, p_dl, p_A, p_B, p_ssm, p_gate, p_mix, p_small = (
            sem(n) for n in ("p_xT", "p_w1", "p_dl", "p_A", "p_B", "p_ssm", "p_gate", "p_mix", "p_small"))
        v_init, v_wlo = sem("v_init"), sem("v_wlo")
        v_xst, v_xag, v_xnlo, v_tap, v_conv, v_xslo = (
            sem(n) for n in ("v_xst", "v_xag", "v_xnlo", "v_tap", "v_conv", "v_xslo"))
        v_cap, v_delta, v_da, v_cum, v_gated, v_h = (
            sem(n) for n in ("v_cap", "v_delta", "v_da", "v_cum", "v_gated", "v_h"))
        v_slo, v_z, v_x1, v_x1st, v_x1ag, v_ext, v_chain = (
            sem(n) for n in ("v_slo", "v_z", "v_x1", "v_x1st", "v_x1ag", "v_ext", "v_chain"))
        held = sem("held")
        v_chain_w, v_chain_g = sem("v_chain_w"), sem("v_chain_g")
        g_chain_0, g_xa, g_xb, g_x1a, g_x1b = (sem(n) for n in ("g_chain_0", "g_xa", "g_xb", "g_x1a", "g_x1b"))
        q_norm, q_T, q_evac, q_clip, q_hi_s, q_lo0, q_lo1, q_y, q_fin = (
            sem(n) for n in ("q_norm", "q_T", "q_evac", "q_clip", "q_hi", "q_lo0", "q_lo1", "q_y", "q_fin"))

        def col(name, m):
            return cols[:, col_at[name] + m:col_at[name] + m + 1]

        def wait(eng, s, value):
            if isinstance(value, int) and value <= 0:
                return
            eng.wait_ge(s, value)

        def nth(n, r, slots):
            return 16 // slots * (n - r) + 16

        def hold(eng):
            eng.sem_inc(held, 1)

        def absent(n):
            return isinstance(n, int) and not 0 <= n < B

        def run_steps(step, eng):
            for t in range(4):
                step(t, t % 2)
            with eng.Fori(2, B // 2 - 1) as i:
                for u in range(2):
                    step(2 * i + u, u)
            for t in range(B - 2, B + 4):
                step(t, t % 2)

        block = ctx.enter_context(nc.Block())

        @block.sync
        def _(sp):
            def load_x(n, r):
                wait(sp, a_xn, n - 1)
                sp.dma_start(x_in[:, r, :, :], x_v[bass.ds(n, 1)].rearrange("o p t d -> (o p) t d")).then_inc(d_x[r], 16)

            sp.dma_start(x_in[:, 0, :, :], x_v[0]).then_inc(d_x[0], 16)
            w_dram = {"w1": w1T, "dl": dlT, "A": AT, "B": BT, "C": CT, "D": DT, "w2": w2T, "w3": w3T}
            for name, _, _ in NAMES:
                sp.dma_start(raw[name], w_dram[name].rearrange("(k p) o -> p k o", p=P)).then_inc(d_w[name], 16)
                if name == "w1":
                    sp.dma_start(cols[:, :], columns).then_inc(d_cols, 16)
                    sp.dma_start(x_in[:, 1, :, :], x_v[1]).then_inc(d_x[1], 16)
            sp.dma_start(raw_ffn[:, :, 0:D], ffn_w.rearrange("(k p) o -> p k o", p=P)).then_inc(d_wf, 16)
            sp.dma_start(g_row[:, :], gamma_row.partition_broadcast(P)).then_inc(d_rows, 16)
            sp.dma_start(b_row[:, :], beta_row.partition_broadcast(P)).then_inc(d_rows, 16)

            def load_residual(n):
                if absent(n):
                    return
                wait(sp, v_x1, 2 * n)
                sp.dma_start(x_res[:, :, :], x_v[bass.ds(n, 1)].rearrange("o p t d -> (o p) t d")).then_inc(d_res, 16)

            def store_x1(n, r):
                if absent(n):
                    return
                sp.wait_ge(g_x1stat, n + 1)
                sp.dma_start(scratch[bass.ds(n, 1)].rearrange("o p f -> (o p) f"),
                             x1[:, r, :, :].rearrange("p t d -> p (t d)")).then_inc(d_store[r], 16)

            def step(t, u):
                load_residual(t - 2)
                if not absent(t + 3):
                    load_x(t + 3, 1 - u)
                store_x1(t - 3, 1 - u)

            step(-1, 1)
            for t in range(4):
                step(t, t % 2)
            with sp.Fori(2, B // 2 - 2) as i:
                for u in range(2):
                    step(2 * i + u, u)
            for t in range(B - 4, B + 3):
                step(t, t % 2)

            def load_x1(n, r):
                wait(sp, q_fin, 2 * (n - R1) + 2)
                sp.dma_start(x1_in[:, r, :, :].rearrange("p t d -> p (t d)"),
                             scratch[bass.ds(n, 1)].rearrange("o p f -> (o p) f")).then_inc(d_x1[r], 16)

            def store(n, r):
                sp.wait_ge(q_fin, 2 * n + 2)
                sp.dma_start(out_v[bass.ds(n, 1)].rearrange("o p t d -> (o p) t d"), y_out[r][:, :, :]).then_inc(d_out[r], 16)

            sp.wait_ge(g_hlo, HD * B)
            sp.wait_ge(a_hhi, HD * B)
            for r in range(2):
                sp.wait_ge(d_store[r], nth(B - 2 + r, r, 2))
            for n in range(R1):
                load_x1(n, n)
            for n in range(R1, 2 * R1):
                store(n - R1, n % 2)
                load_x1(n, n % R1)
            with sp.Fori(2, B // 4) as i:
                for r in range(4):
                    store(4 * i + (r - R1), r % 2)
                    load_x1(4 * i + r, r)
            for n in range(B - R1, B):
                store(n, n % 2)
            for r in range(2):
                sp.wait_ge(d_out[r], nth(B - 2 + r, r, 2))

        @block.tensor
        def _(pe):
            def product(bank, name, m, x_hi, x_lo, first=True, last=True):
                kt = w_hi[name].shape[1]
                for k in range(kt):
                    hi = w_hi[name][:, k, m * P:(m + 1) * P]
                    lo = w_lo[name][:, k, m * P:(m + 1) * P]
                    pe.matmul(bank, hi, x_hi[:, k, :], start=(first and k == 0), stop=False)
                    pe.matmul(bank, hi, x_lo[:, k, :], start=False, stop=False)
                    done = pe.matmul(bank, lo, x_hi[:, k, :], start=False, stop=(last and k == kt - 1))
                return done

            def hidden_product(n, r, j, k):
                if absent(n):
                    return
                q = HD * n + j
                if isinstance(n, int) and n == 0:
                    pe.wait_ge(v_wlo, 4)
                if k == 0 and j == 0:
                    pe.wait_ge(v_xslo, CD * n + CD)
                wait(pe, (v_delta, v_da, v_gated)[k], q - 1)
                product(hb[:, 3 * (j % 2) + k, :], ("dl", "A", "B")[k], j, xs_hi[:, r], xs_lo[:, r]).then_inc(
                    (p_dl, p_A, p_B)[k], 1)

            def transpose_x(n, c):
                if absent(n):
                    return
                if isinstance(n, int) and n == 0:
                    pe.wait_ge(g_const, 1)
                if c == 0:
                    pe.wait_ge(a_xn, n + 1)
                if absent(n - 3):
                    wait(pe, v_conv, CD * (n - 1) + c + 1)
                else:
                    pe.wait_ge(v_x1, 2 * (n - 3) + c + 1)
                for i in range(TT):
                    done = pe.transpose(mb[:, c, i * P:(i + 1) * P], xn[:, i, c * P:(c + 1) * P], ident[:, :])
                done.then_inc(p_xT, 1)

            def front_product(n, m):
                if absent(n):
                    return
                if isinstance(n, int) and n == 0:
                    pe.wait_ge(v_wlo, 1)
                if m == 0:
                    pe.wait_ge(v_xnlo, CD * n + CD)
                if not absent(n - 2):
                    pe.wait_ge(a_gate, CD * (n - 2) + m + 1)
                product(mb[:, m, :], "w1", m, xn_hi, xn_lo).then_inc(p_w1, 1)

            def ssm_product(n, r, m):
                if absent(n):
                    return
                if m == 0:
                    if isinstance(n, int) and n == 0:
                        pe.wait_ge(v_wlo, len(NAMES))
                        pe.wait_ge(v_init, 1)
                    pe.wait_ge(a_hhi, HD * n + HD)
                    pe.wait_ge(g_hlo, HD * n + HD)
                if absent(n + 2):
                    pe.wait_ge(v_x1, 2 * (n - 1) + m + 1)
                else:
                    pe.wait_ge(v_xnlo, CD * (n + 2) + m + 1)
                product(mb[:, m, :], "D", m, xs_hi[:, r], xs_lo[:, r], last=False)
                product(mb[:, m, :], "C", m, h_hi[:, r], h_lo[:, r], first=False).then_inc(p_ssm, 1)

            def gate_product(n, m):
                if absent(n):
                    return
                pe.wait_ge(v_slo, CD * n + CD)
                product(mb[:, m, :], "w2", m, s_hi, s_lo).then_inc(p_gate, 1)

            def mix(n, half):
                if absent(n):
                    return
                if half == 0:
                    pe.wait_ge(a_zhi, CD * n + CD)
                    pe.wait_ge(g_zlo, CD * n + CD)
                if not absent(n + 2):
                    pe.wait_ge(v_conv, CD * (n + 2) + half + 1)
                for e in range(2):
                    acc = mb[:, half, e * D:(e + 1) * D]
                    tok = slice((2 * half + e) * P, (2 * half + e + 1) * P)
                    for k in range(CD):
                        pe.matmul(acc, z_hi[:, k, tok], w_hi["w3"][:, k, :], start=(k == 0), stop=False)
                        pe.matmul(acc, z_hi[:, k, tok], w_lo["w3"][:, k, :], start=False, stop=False)
                        pe.matmul(acc, z_lo[:, k, tok], w_hi["w3"][:, k, :], start=False, stop=(k == CD - 1))
                    for k in range(CD):
                        part = mb[:, half, e * D + k * P:e * D + (k + 1) * P]
                        pe.matmul(part, s_hi[:, k, tok], ident_r[:, :], start=False, stop=True, skip_group_check=True)
                        done = pe.matmul(part, s_lo[:, k, tok], ident_r[:, :], start=False, stop=True,
                                         skip_group_check=True)
                done.then_inc(p_mix, 1)

            def step(t, u):
                DL, A, B_ = 0, 1, 2
                hidden_product(t - 1, 1 - u, 0, DL)
                transpose_x(t, 0)
                hidden_product(t - 1, 1 - u, 1, DL)
                hidden_product(t - 1, 1 - u, 0, A)
                hidden_product(t - 1, 1 - u, 0, B_)
                hidden_product(t - 1, 1 - u, 1, A)
                transpose_x(t, 1)
                hidden_product(t - 1, 1 - u, 2, DL)
                ssm_product(t - 2, u, 0)
                ssm_product(t - 2, u, 1)
                hidden_product(t - 1, 1 - u, 3, DL)
                hidden_product(t - 1, 1 - u, 2, A)
                gate_product(t - 2, 0)
                gate_product(t - 2, 1)
                hidden_product(t - 1, 1 - u, 1, B_)
                front_product(t, 0)
                front_product(t, 1)
                hidden_product(t - 1, 1 - u, 2, B_)
                hidden_product(t - 1, 1 - u, 3, B_)
                hidden_product(t - 1, 1 - u, 3, A)
                mix(t - 2, 0)
                mix(t - 2, 1)

            pe.wait_ge(v_init, 2)
            pe.wait_ge(g_const, 1)
            pe.matmul(hb[:, 5, 0:1], ones[:, :], scal[:, 0:1], start=True, stop=True).then_inc(p_small, 1)
            pe.wait_ge(v_init, 3)

            run_steps(step, pe)

            pe.wait_ge(v_chain, 1)
            pe.transpose(hb[0:1, 0, 0:P], scal[:, 1:2], ident[:, :]).then_inc(p_small, 1)
            pe.wait_ge(v_chain, 2)
            pe.matmul(hb[:, 1, 0:1], ones[0:1, :], scal[0:1, 2:3], start=True, stop=True).then_inc(p_small, 1)

            def y_bank(r, half):
                return hb[:, 4 + half, :] if r == 0 else mb[:, half, :]

            def transposes(n, r):
                pe.wait_ge(q_norm, n + 1)
                wait(pe, q_evac, CD * (n - 1))
                for c in range(CD):
                    for i in range(TT):
                        done = pe.transpose(hb[:, 2 * r + c, i * P:(i + 1) * P], xn2[:, r, i, c * P:(c + 1) * P], ident[:, :])
                    done.then_inc(q_T, 1)

            def projection(n, r):
                pe.wait_ge(q_lo0, n + 1)
                pe.wait_ge(q_lo1, n + 1)
                wait(pe, q_fin, 2 * (n - 1))
                for i in range(TT):
                    acc = y_bank(r, i // 2)[:, (i % 2) * D:(i % 2 + 1) * D]
                    tok = slice(i * P, (i + 1) * P)
                    for k in range(CD):
                        pe.matmul(acc, q_hi[:, r, k, tok], wq[:, k, :], start=(k == 0), stop=False)
                        done = pe.matmul(acc, q_lo[:, r, k, tok], wq[:, k, :], start=False, stop=(k == CD - 1))
                    if i % 2 == 1:
                        done.then_inc(q_y, 1)

            pe.wait_ge(v_chain, 3)
            transposes(0, 0)
            for n in range(2):
                transposes(n + 1, 1 - n)
                projection(n, n)
            with pe.Fori(1, B // 2 - 1) as i:
                for u in range(2):
                    transposes(2 * i + u + 1, 1 - u)
                    projection(2 * i + u, u)
            transposes(B - 1, 1)
            projection(B - 2, 0)
            projection(B - 1, 1)

        @block.scalar
        def _(act):
            act.preload_act_table_set(EXP_LN_TABLE)

            def split_hi_of(name):
                act.wait_ge(d_w[name], 16)
                act.activation(w_hi[name][:, :, :], raw[name], ACT.Copy).then_inc(a_whi, 1)

            split_hi_of(NAMES[0][0])

            def exp_u(n, j):
                if absent(n):
                    return
                if isinstance(n, int) and n == 0:
                    act.wait_ge(v_wlo, len(NAMES))
                act.wait_ge(p_dl, HD * n + j + 1)
                act.activation(softp[:, j % 2, :], hb[:, 3 * (j % 2), :], ACT.Exp, bias=col("dl_b", j)).then_inc(a_exp, 1)

            def ln_1p(n, j):
                if absent(n):
                    return
                act.wait_ge(v_cap, HD * n + j + 1)
                act.activation(softp[:, j % 2, :], softp[:, j % 2, :], ACT.Ln, bias=1.0).then_inc(a_ln, 1)

            def decay(n, j):
                if absent(n):
                    return
                act.wait_ge(v_cum, HD * n + j + 1)
                act.activation(cumul[:, j % 2, :], cumul[:, j % 2, :], ACT.Exp, scale=-1.0).then_inc(a_decay, 1)

            def hidden_hi(n, r, j):
                if absent(n):
                    return
                act.wait_ge(v_h, HD * n + j + 1)
                if j == 0:
                    wait(act, p_ssm, CD * (n - 1))
                act.activation(h_hi[:, r, j, :], hsum[:, j % 2, :], ACT.Copy).then_inc(a_hhi, 1)

            def normalise_x(n, r):
                if absent(n):
                    return
                act.wait_ge(g_xnorm, n + 1)
                wait(act, p_xT, CD * n)
                for i in range(TT):
                    done = act.activation(xn[:, i, :], x_in[:, r, i, :], ACT.Identity, scale=x_norm[:, 0, i:i + 1],
                                          bias=x_norm[:, 1, i:i + 1])
                done.then_inc(a_xn, 1)

            def xn_hi_of(n, c):
                if absent(n):
                    return
                act.wait_ge(p_xT, CD * n + c + 1)
                wait(act, p_w1, CD * n)
                act.activation(xn_hi[:, c, :], mb[:, c, :], ACT.Copy).then_inc(a_xnhi, 1)

            def centre_tap(n, c):
                if absent(n):
                    return
                if isinstance(n, int) and n == 0:
                    act.wait_ge(d_cols, 16)
                act.wait_ge(p_w1, CD * n + c + 1)
                wait(act, v_xslo, CD * (n - 1) + c + 1)
                act.activation(xs[:, c, :], mb[:, c, :], ACT.Identity, scale=col("conv_w1", c),
                               bias=col("conv_b", c)).then_inc(a_tap, 1)

            def silu_x(n, c):
                if absent(n):
                    return
                act.wait_ge(v_conv, CD * n + c + 1)
                act.activation(xs[:, c, :], xs[:, c, :], ACT.Silu).then_inc(a_xs, 1)

            def x_hi_of(n, r, c):
                if absent(n):
                    return
                act.wait_ge(a_xs, CD * n + c + 1)
                wait(act, p_ssm, CD * (n - 1))
                act.activation(xs_hi[:, r, c, :], xs[:, c, :], ACT.Copy).then_inc(a_xshi, 1)

            def ssm_out(n, m, hi):
                if absent(n):
                    return
                if isinstance(n, int) and n == 0:
                    act.wait_ge(v_init, 4)
                act.wait_ge(p_ssm, CD * n + m + 1)
                wait(act, p_mix, 2 * n)
                out_, done = (s_hi, a_shi) if hi else (s_buf, a_s)
                act.activation(out_[:, m, :], mb[:, m, :], ACT.Identity, bias=cd_b[:, m:m + 1]).then_inc(done, 1)

            def silu_gate(n, m):
                if absent(n):
                    return
                act.wait_ge(p_gate, CD * n + m + 1)
                act.activation(gate[:, m, :], mb[:, m, :], ACT.Silu).then_inc(a_gate, 1)

            def z_hi_of(n, m):
                if absent(n):
                    return
                act.wait_ge(v_z, CD * n + m + 1)
                act.activation(z_hi[:, m, :], z_buf[:, m, :], ACT.Copy).then_inc(a_zhi, 1)

            def normalise_x1(n, r):
                if absent(n):
                    return
                act.wait_ge(g_x1stat, n + 1)
                act.wait_ge(v_ext, n + 1)
                for i in range(TT):
                    done = act.activation(x1n[:, i, :], x1[:, r, i, 0:D], ACT.Identity,
                                          scale=x1[:, r, i, D:D + 1], bias=x1[:, r, i, D + 1:D + 2])
                done.then_inc(a_x1n, 1)

            normalise_x(0, 0)
            for name, _, _ in NAMES[1:]:
                split_hi_of(name)

            def step(t, u):
                exp_u(t - 1, 0)
                exp_u(t - 1, 1)
                ln_1p(t - 1, 0)
                xn_hi_of(t, 0)
                hidden_hi(t - 2, u, 3)
                xn_hi_of(t, 1)
                exp_u(t - 1, 2)
                decay(t - 1, 0)
                normalise_x(t + 1, 1 - u)
                ln_1p(t - 1, 1)
                ssm_out(t - 2, 0, False)
                ln_1p(t - 1, 2)
                ssm_out(t - 2, 0, True)
                ssm_out(t - 2, 1, True)
                ssm_out(t - 2, 1, False)
                decay(t - 1, 1)
                exp_u(t - 1, 3)
                hidden_hi(t - 1, 1 - u, 0)
                ln_1p(t - 1, 3)
                silu = not (absent(t) and absent(t - 2))
                if silu:
                    act.preload_act_table_set(SILU_TABLE)
                silu_gate(t - 2, 0)
                silu_gate(t - 2, 1)
                z_hi_of(t - 2, 0)
                centre_tap(t, 0)
                z_hi_of(t - 2, 1)
                centre_tap(t, 1)
                silu_x(t, 0)
                silu_x(t, 1)
                x_hi_of(t, u, 0)
                x_hi_of(t, u, 1)
                if silu:
                    act.preload_act_table_set(EXP_LN_TABLE)
                decay(t - 1, 2)
                hidden_hi(t - 1, 1 - u, 1)
                normalise_x1(t - 3, 1 - u)
                decay(t - 1, 3)
                hidden_hi(t - 1, 1 - u, 2)

            run_steps(step, act)

            act.wait_ge(v_chain, 4)

            def evacuate(n, r):
                for c in range(CD):
                    act.wait_ge(q_T, CD * n + c + 1)
                    wait(act, q_lo1, n - 1)
                    wait(act, q_lo0, n - 1)
                    act.activation(xc[r][:, c, :], hb[:, 2 * r + c, :], ACT.Identity, scale=scal[:, 6 + c:7 + c],
                                   bias=scal[:, 8 + c:9 + c]).then_inc(q_evac, 1)

            def split_hi(n, r):
                wait(act, q_y, 2 * (n - 1))
                for c in range(CD):
                    act.wait_ge(q_clip, CD * n + c + 1)
                    act.activation(q_hi[:, r, c, :], xc[r][:, c, :], ACT.Copy).then_inc(q_hi_s, 1)

            evacuate(0, 0)
            for n in range(2):
                split_hi(n, n)
                evacuate(n + 1, 1 - n)
            with act.Fori(1, B // 2 - 1) as i:
                for u in range(2):
                    split_hi(2 * i + u, u)
                    evacuate(2 * i + u + 1, 1 - u)
            split_hi(B - 2, 0)
            evacuate(B - 1, 1)
            split_hi(B - 1, 1)

        @block.vector
        def _(dve):
            def raw_f32(ap):
                return ap.bitcast(F32)

            def x_stats(n, r):
                if absent(n):
                    return
                wait(dve, v_xag, n)
                dve.wait_ge(d_x[r], nth(n, r, 2))
                for i in range(TT):
                    done = dve.bn_stats(x_stat[:, i, :], x_in[:, r, i, :])
                done.then_inc(v_xst, 1)

            def x_aggregate(n):
                if absent(n):
                    return
                wait(dve, g_xnorm, n)
                dve.wait_ge(v_xst, n + 1)
                hold(dve)
                for i in range(TT):
                    done = dve.bn_aggr(x_mv[:, i, :], x_stat[:, i, :])
                done.then_inc(v_xag, 1)

            x_stats(0, 0)
            x_aggregate(0)
            x_stats(1, 1)

            def split_weight(k, name):
                dve.wait_ge(a_whi, k + 1)
                dve.tensor_tensor(w_lo[name][:, :, :], raw[name], raw_f32(w_hi[name][:, :, :]), ALU.subtract).then_inc(v_wlo, 1)

            split_weight(0, "w1")
            for k, (name, _, _) in enumerate(NAMES[1:4]):
                split_weight(k + 1, name)
            dve.wait_ge(g_const, 1)
            dve.tensor_copy(ident_r[:, :], ident[:, :]).then_inc(v_init, 1)
            dve.wait_ge(d_wf, 16)
            dve.tensor_reduce(scal[:, 0:1], raw_ffn[:, :, 0:D], AX.XY, ALU.add, apply_absolute_value=True).then_inc(v_init, 1)
            dve.wait_ge(p_small, 1)
            dve.tensor_scalar(scal[:, 3:4], hb[:, 5, 0:1], 1.0 / (D * D), None, ALU.mult).then_inc(v_chain_w, 1)
            dve.wait_ge(v_chain_w, 1)
            dve.tensor_scalar(scal[:, 4:5], scal[:, 3:4], Q_EPS, None, ALU.add).then_inc(v_chain_w, 1)
            dve.wait_ge(v_chain_w, 2)
            dve.reciprocal(scal[:, 5:6], scal[:, 4:5]).then_inc(v_chain_w, 1)
            dve.wait_ge(v_chain_w, 3)
            wf = raw_ffn[:, :, 0:D]
            dve.tensor_scalar(wf, wf, scal[:, 5:6], ROUND_MAGIC, ALU.mult, ALU.add).then_inc(v_chain_w, 1)
            dve.wait_ge(v_chain_w, 4)
            dve.tensor_scalar(wf, wf, ROUND_MAGIC, 1.0, ALU.subtract, ALU.min).then_inc(v_chain_w, 1)
            dve.wait_ge(v_chain_w, 5)
            dve.tensor_scalar(wq[:, :, :], wf, -1.0, None, ALU.max).then_inc(v_init, 1)
            for k, (name, _, _) in enumerate(NAMES[4:]):
                split_weight(k + 4, name)
            dve.wait_ge(d_cols, 16)
            dve.tensor_tensor(cd_b[:, :], cols[:, col_at["C_b"]:col_at["C_b"] + CD],
                              cols[:, col_at["D_b"]:col_at["D_b"] + CD], ALU.add).then_inc(v_init, 1)
            dve.memset(hi_run[:, :, :], -BIG)
            dve.memset(lo_run[:, :, :], BIG).then_inc(v_ext, 1)

            def cap(n, j):
                if absent(n):
                    return
                q = HD * n + j
                dve.wait_ge(a_exp, q + 1)
                dve.tensor_scalar(softp[:, j % 2, :], softp[:, j % 2, :], EXP_CAP, None, ALU.min).then_inc(v_cap, 1)

            def delta_of(n, j):
                if absent(n):
                    return
                q = HD * n + j
                dve.wait_ge(a_ln, q + 1)
                dve.scalar_tensor_tensor(out=delta[:, j % 2, :], in0=hb[:, 3 * (j % 2), :], scalar=col("dl_b", j),
                                         in1=softp[:, j % 2, :], op0=ALU.add, op1=ALU.max).then_inc(v_delta, 1)

            def delta_A(n, j):
                if absent(n):
                    return
                q = HD * n + j
                dve.wait_ge(p_A, q + 1)
                dve.wait_ge(v_delta, q + 1)
                dve.scalar_tensor_tensor(out=delta[:, j % 2, :], in0=hb[:, 3 * (j % 2) + 1, :], scalar=col("A_b", j),
                                         in1=delta[:, j % 2, :], op0=ALU.add, op1=ALU.mult).then_inc(v_da, 1)

            def decay_sum(n, j):
                if absent(n):
                    return
                dve.wait_ge(v_da, HD * n + j + 1)
                dve.tensor_tensor_scan(out=cumul[:, j % 2, :], data0=delta[:, j % 2, :], data1=delta[:, j % 2, :],
                                       initial=0.0, op0=ALU.add, op1=ALU.bypass).then_inc(v_cum, 1)

            def gated_B(n, j):
                if absent(n):
                    return
                q = HD * n + j
                dve.wait_ge(p_B, q + 1)
                dve.wait_ge(a_decay, q + 1)
                wait(dve, a_hhi, q - 1)
                wait(dve, g_hlo, q - 1)
                dve.scalar_tensor_tensor(out=gated[:, j % 2, :], in0=hb[:, 3 * (j % 2) + 2, :], scalar=col("B_b", j),
                                         in1=cumul[:, j % 2, :], op0=ALU.add, op1=ALU.mult).then_inc(v_gated, 1)

            def hidden_state(n, j):
                if absent(n):
                    return
                dve.wait_ge(v_gated, HD * n + j + 1)
                dve.tensor_tensor_scan(out=hsum[:, j % 2, :], data0=gated[:, j % 2, :], data1=gated[:, j % 2, :],
                                       initial=0.0, op0=ALU.add, op1=ALU.bypass).then_inc(v_h, 1)

            def split_s(n, m):
                if absent(n):
                    return
                dve.wait_ge(a_s, CD * n + m + 1)
                dve.wait_ge(a_shi, CD * n + m + 1)
                dve.tensor_tensor(s_lo[:, m, :], s_buf[:, m, :], raw_f32(s_hi[:, m, :]), ALU.subtract).then_inc(v_slo, 1)

            def extrema(n):
                if absent(n):
                    return
                dve.wait_ge(a_x1n, n + 1)
                dve.wait_ge(v_ext, n + 1)
                dve.tensor_tensor(hi_run[:, :, :], hi_run[:, :, :], x1n[:, :, :], ALU.max)
                dve.tensor_tensor(lo_run[:, :, :], lo_run[:, :, :], x1n[:, :, :], ALU.min).then_inc(v_ext, 1)

            def xn_lo_of(n, c):
                if absent(n):
                    return
                dve.wait_ge(a_xnhi, CD * n + c + 1)
                dve.tensor_tensor(xn_lo[:, c, :], mb[:, c, :], raw_f32(xn_hi[:, c, :]), ALU.subtract).then_inc(v_xnlo, 1)

            def left_tap(n, c):
                if absent(n):
                    return
                dve.wait_ge(a_tap, CD * n + c + 1)
                dve.scalar_tensor_tensor(out=xs[:, c, 1:L], in0=mb[:, c, 0:L - 1], scalar=col("conv_w0", c),
                                         in1=xs[:, c, 1:L], op0=ALU.mult, op1=ALU.add).then_inc(v_tap, 1)

            def right_tap(n, c):
                if absent(n):
                    return
                dve.wait_ge(v_tap, CD * n + c + 1)
                dve.scalar_tensor_tensor(out=xs[:, c, 0:L - 1], in0=mb[:, c, 1:L], scalar=col("conv_w2", c),
                                         in1=xs[:, c, 0:L - 1], op0=ALU.mult, op1=ALU.add).then_inc(v_conv, 1)

            def x_lo_of(n, r, c):
                if absent(n):
                    return
                dve.wait_ge(a_xshi, CD * n + c + 1)
                dve.tensor_tensor(xs_lo[:, r, c, :], xs[:, c, :], raw_f32(xs_hi[:, r, c, :]), ALU.subtract).then_inc(v_xslo, 1)

            def gated_ssm(n, m):
                if absent(n):
                    return
                dve.wait_ge(a_gate, CD * n + m + 1)
                dve.wait_ge(a_s, CD * n + m + 1)
                wait(dve, g_zlo, CD * (n - 1) + m + 1)
                wait(dve, a_zhi, CD * (n - 1) + m + 1)
                dve.tensor_tensor(z_buf[:, m, :], gate[:, m, :], s_buf[:, m, :], ALU.mult).then_inc(v_z, 1)

            def add_residual(n, r, half):
                if absent(n):
                    return
                if half == 0:
                    dve.wait_ge(d_res, 16 * n + 16)
                    wait(dve, d_store[r], nth(n - 2, r, 2))
                    wait(dve, a_x1n, n - 1)
                dve.wait_ge(p_mix, 2 * n + half + 1)
                dve.tensor_tensor(x1[:, r, 2 * half:2 * half + 2, 0:D], x_res[:, 2 * half:2 * half + 2, :],
                                  mb[:, half, :].rearrange("p (t d) -> p t d", t=2), ALU.add).then_inc(v_x1, 1)

            def x1_stats(n, r):
                if absent(n):
                    return
                wait(dve, v_x1ag, n)
                dve.wait_ge(v_x1, 2 * n + 2)
                for i in range(TT):
                    done = dve.bn_stats(x1_stat[:, i, :], x1[:, r, i, 0:D])
                done.then_inc(v_x1st, 1)

            def x1_aggregate(n):
                if absent(n):
                    return
                wait(dve, g_x1stat, n)
                dve.wait_ge(v_x1st, n + 1)
                hold(dve)
                for i in range(TT):
                    done = dve.bn_aggr(x1_mv[:, i, :], x1_stat[:, i, :])
                done.then_inc(v_x1ag, 1)

            def step(t, u):
                gated_B(t - 2, 3)
                x_aggregate(t + 1)
                cap(t - 1, 0)
                hidden_state(t - 2, 3)
                cap(t - 1, 1)
                delta_of(t - 1, 0)
                xn_lo_of(t, 0)
                delta_A(t - 1, 0)
                x_stats(t + 2, u)
                xn_lo_of(t, 1)
                decay_sum(t - 1, 0)
                extrema(t - 4)
                cap(t - 1, 2)
                gated_B(t - 1, 0)
                delta_of(t - 1, 1)
                hidden_state(t - 1, 0)
                delta_A(t - 1, 1)
                split_s(t - 2, 0)
                decay_sum(t - 1, 1)
                split_s(t - 2, 1)
                x1_stats(t - 3, 1 - u)
                delta_of(t - 1, 2)
                cap(t - 1, 3)
                delta_A(t - 1, 2)
                gated_ssm(t - 2, 0)
                decay_sum(t - 1, 2)
                gated_ssm(t - 2, 1)
                gated_B(t - 1, 1)
                x1_aggregate(t - 3)
                delta_of(t - 1, 3)
                left_tap(t, 0)
                left_tap(t, 1)
                right_tap(t, 0)
                right_tap(t, 1)
                hidden_state(t - 1, 1)
                delta_A(t - 1, 3)
                x_lo_of(t, u, 0)
                x_lo_of(t, u, 1)
                add_residual(t - 2, u, 0)
                gated_B(t - 1, 2)
                decay_sum(t - 1, 3)
                hidden_state(t - 1, 2)
                add_residual(t - 2, u, 1)

            run_steps(step, dve)

            count = [0]

            def chained(ins):
                count[0] += 1
                ins.then_inc(v_chain_g, 1)
                dve.wait_ge(v_chain_g, count[0])

            dve.wait_ge(v_ext, B + 1)
            dve.wait_ge(d_rows, 32)
            ext = [x_in[:, 0, 0, :], x_in[:, 0, 1, :]]
            chained(dve.tensor_reduce(ext[0], hi_run[:, :, :].rearrange("p t d -> p d t"), AX.X, ALU.max))
            chained(dve.tensor_reduce(ext[1], lo_run[:, :, :].rearrange("p t d -> p d t"), AX.X, ALU.min))
            for e in ext:
                chained(dve.tensor_tensor(e, e, g_row[:, :], ALU.mult))
                chained(dve.tensor_tensor(e, e, b_row[:, :], ALU.add))
            dve.tensor_reduce(scal[:, 1:2], x_in[:, 0, 0:2, :], AX.XY, ALU.max, apply_absolute_value=True).then_inc(v_chain, 1)
            dve.wait_ge(p_small, 2)
            dve.reduce_max(scal[0:1, 2:3], hb[0:1, 0, 0:P], axis=AX.X).then_inc(v_chain, 1)
            dve.wait_ge(p_small, 3)
            dve.tensor_copy(scal[:, 10:11], hb[:, 1, 0:1]).then_inc(v_chain, 1)
            dve.wait_ge(v_chain, 3)
            chained(dve.reciprocal(scal[:, 11:12], scal[:, 10:11]))
            chained(dve.tensor_scalar(scal[:, 12:13], scal[:, 11:12], QB, None, ALU.mult))
            chained(dve.tensor_scalar(scal[:, 13:14], scal[:, 10:11], scal[:, 3:4], 1.0 / QB, ALU.mult, ALU.mult))
            chained(dve.tensor_scalar(scal[:, 6:8], cols[:, col_at["ln_gamma"]:col_at["ln_gamma"] + CD],
                                      scal[:, 12:13], None, ALU.mult))
            dve.tensor_scalar(scal[:, 8:10], cols[:, col_at["ln_beta"]:col_at["ln_beta"] + CD],
                              scal[:, 12:13], None, ALU.mult).then_inc(v_chain, 1)

            def normalise(n, r, r4):
                dve.wait_ge(d_x1[r4], nth(n, r4, 4))
                wait(dve, q_T, CD * (n - 1))
                for i in range(TT):
                    done = dve.tensor_scalar(xn2[:, r, i, :], x1_in[:, r4, i, 0:D], x1_in[:, r4, i, D:D + 1],
                                             x1_in[:, r4, i, D + 1:D + 2], ALU.mult, ALU.add)
                done.then_inc(q_norm, 1)

            def clip(n, r):
                for c in range(CD):
                    dve.wait_ge(q_evac, CD * n + c + 1)
                    dve.tensor_scalar(xc[r][:, c, :], xc[r][:, c, :], CLIP, -CLIP, ALU.min, ALU.max).then_inc(q_clip, 1)

            def split_lo(n, r):
                dve.wait_ge(q_hi_s, CD * n + 2)
                dve.tensor_tensor(q_lo[:, r, 1, :], xc[r][:, 1, :], raw_f32(q_hi[:, r, 1, :]), ALU.subtract).then_inc(q_lo1, 1)

            def finish(n, r, r4):
                wait(dve, d_out[r], nth(n - 2, r, 2))
                for half in range(2):
                    dve.wait_ge(q_y, 2 * n + half + 1)
                    src = hb[:, 4 + half, :] if r == 0 else mb[:, half, :]
                    dve.scalar_tensor_tensor(out=y_out[r][:, 2 * half:2 * half + 2, :], in0=src.rearrange("p (t d) -> p t d", t=2),
                                             scalar=scal[:, 13:14], in1=x1_in[:, r4, 2 * half:2 * half + 2, 0:D],
                                             op0=ALU.mult, op1=ALU.add).then_inc(q_fin, 1)

            dve.wait_ge(v_chain, 4)
            normalise(0, 0, 0)

            def step2(t, u, u4, before, after):
                if after:
                    normalise(t + 1, 1 - u, (u4 + 1) % 4)
                clip(t, u)
                if before:
                    finish(t - 1, 1 - u, (u4 + 3) % 4)
                split_lo(t, u)

            for t in range(4):
                step2(t, t % 2, t, t > 0, True)
            with dve.Fori(1, B // 4 - 1) as i:
                for u4 in range(4):
                    step2(4 * i + u4, u4 % 2, u4, True, True)
            for t in range(B - 4, B):
                step2(t, t % 2, t % 4, True, t + 1 < B)
            finish(B - 1, 1, 3)

        @block.gpsimd
        def _(pool):
            chain = [0]

            def chained(ins):
                chain[0] += 1
                ins.then_inc(g_chain_0, 1)
                pool.wait_ge(g_chain_0, chain[0])

            chained(pool.memset(ident[:, :], 0.0))
            chained(pool.memset(ones[:, :], 1.0))
            chained(pool.memset(neg_half[:, :], -0.5))
            pool.affine_select(out=ident[:, :], in_=ident[:, :], compare_op=ALU.not_equal, fill=1.0, base=0,
                               pattern=[[-1, P]], channel_multiplier=1).then_inc(g_const, 1)

            def x_norm_of(n):
                if absent(n):
                    return
                pool.wait_ge(v_xag, n + 1)
                wait(pool, a_xn, n)
                hold(pool)
                pool.tensor_scalar(x_tmp[:, 0, :], x_mv[:, :, 1], LN_EPS, None, ALU.add).then_inc(g_xa, 1)
                pool.tensor_scalar(x_tmp[:, 1, :], x_mv[:, :, 0], -1.0, 0.0, ALU.mult, ALU.add).then_inc(g_xa, 1)
                pool.wait_ge(g_xa, 2 * n + 2)
                pool.tensor_tensor(x_norm[:, 0, :], x_tmp[:, 0, :], neg_half[:, :], ALU.pow).then_inc(g_xb, 1)
                pool.wait_ge(g_xb, n + 1)
                pool.tensor_tensor(x_norm[:, 1, :], x_tmp[:, 1, :], x_norm[:, 0, :], ALU.mult).then_inc(g_xnorm, 1)

            def x1_norm_of(n, r):
                if absent(n):
                    return
                pool.wait_ge(v_x1ag, n + 1)
                hold(pool)
                pool.tensor_scalar(x1_tmp[:, 0, :], x1_mv[:, :, 1], 1.0 + FFN_LN_EPS, LN_EPS * FFN_LN_EPS,
                                   ALU.mult, ALU.add).then_inc(g_x1a, 1)
                pool.tensor_scalar(x1_tmp[:, 1, :], x1_mv[:, :, 0], -1.0, 0.0, ALU.mult, ALU.add).then_inc(g_x1a, 1)
                pool.wait_ge(g_x1a, 2 * n + 2)
                pool.tensor_tensor(x1[:, r, :, D], x1_tmp[:, 0, :], neg_half[:, :], ALU.pow).then_inc(g_x1b, 1)
                pool.wait_ge(g_x1b, n + 1)
                pool.tensor_tensor(x1[:, r, :, D + 1], x1_tmp[:, 1, :], x1[:, r, :, D], ALU.mult).then_inc(g_x1stat, 1)

            def hidden_lo(n, r, j):
                if absent(n):
                    return
                pool.wait_ge(a_hhi, HD * n + j + 1)
                if j == 0:
                    wait(pool, p_ssm, CD * (n - 1))
                pool.tensor_tensor(h_lo[:, r, j, :], hsum[:, j % 2, :], h_hi[:, r, j, :].bitcast(F32),
                                   ALU.subtract).then_inc(g_hlo, 1)

            def z_lo_of(n, m):
                if absent(n):
                    return
                pool.wait_ge(a_zhi, CD * n + m + 1)
                wait(pool, p_mix, 2 * n)
                pool.tensor_tensor(z_lo[:, m, :], z_buf[:, m, :], z_hi[:, m, :].bitcast(F32), ALU.subtract).then_inc(g_zlo, 1)

            x_norm_of(0)

            def step(t, u):
                hidden_lo(t - 2, u, 3)
                x_norm_of(t + 1)
                z_lo_of(t - 2, 0)
                hidden_lo(t - 1, 1 - u, 0)
                z_lo_of(t - 2, 1)
                x1_norm_of(t - 3, 1 - u)
                hidden_lo(t - 1, 1 - u, 1)
                hidden_lo(t - 1, 1 - u, 2)

            run_steps(step, pool)

            def split_lo(n, r):
                pool.wait_ge(q_hi_s, CD * n + 1)
                pool.tensor_tensor(q_lo[:, r, 0, :], xc[r][:, 0, :], q_hi[:, r, 0, :].bitcast(F32),
                                   ALU.subtract).then_inc(q_lo0, 1)

            with pool.Fori(0, B // 2) as i:
                for u in range(2):
                    split_lo(2 * i + u, u)


def kernel(**inputs):
    import concourse.bacc as _bacc
    from concourse.bass_utils import run_bass_kernel_spmd as _run

    a = {k.split("L0_")[1]: np.asarray(v) for k, v in inputs.items()}
    D, H = a["attn_w1"].shape[0], a["attn_A_w"].shape[0]

    def tiles(v):
        return np.ascontiguousarray(v.reshape(-1, P).T)

    conv = a["attn_conv_w"].reshape(D, 3)
    named = {"dl_b": a["attn_dl_b"], "A_b": a["attn_A_b"], "B_b": a["attn_B_b"], "C_b": a["attn_C_b"],
             "D_b": a["attn_D_b"], "conv_b": a["attn_conv_b"], "conv_w0": conv[:, 0], "conv_w1": conv[:, 1],
             "conv_w2": conv[:, 2], "ln_gamma": a["ffn_ln_gamma"], "ln_beta": a["ffn_ln_beta"]}
    where, _ = column_layout(D, H)
    columns = np.concatenate([tiles(named[n]) for n in where], axis=1)
    arrays = {"x": a["attn_x"], "w1T": a["attn_w1"].T, "w2T": a["attn_w2"].T, "w3T": a["attn_w3"].T,
              "dlT": a["attn_dl_w"].T, "AT": a["attn_A_w"].T, "BT": a["attn_B_w"].T, "CT": a["attn_C_w"].T,
              "DT": a["attn_D_w"].T, "ffn_w": a["ffn_weight"], "columns": columns,
              "gamma_row": a["ffn_ln_gamma"], "beta_row": a["ffn_ln_beta"]}
    arrays = {k: np.ascontiguousarray(v) for k, v in arrays.items()}

    nc = _bacc.Bacc("TRN2", target_bir_lowering=False, num_devices=1)
    args = [nc.dram_tensor(k, v.shape, mybir.dt.from_np(v.dtype), kind="ExternalInput").ap() for k, v in arrays.items()]
    out = nc.dram_tensor("out", a["attn_x"].shape, F32, kind="ExternalOutput").ap()
    build(nc, *args, out)
    r = _run(nc, [arrays], core_ids=[0])
    return r.results[0]["out"]
```

```python
from contextlib import ExitStack

import numpy as np

import concourse.bass as bass
from concourse import mybir

P = 128
F32 = mybir.dt.float32
F32R = mybir.dt.float32r
ALU = mybir.AluOpType
ACT = mybir.ActivationFunctionType
AX = mybir.AxisListType

LN_EPS = 1e-5
FFN_LN_EPS = 1e-3
QB = 128.0
Q_EPS = 1e-5
CLIP = float(np.float32(QB - Q_EPS))
ROUND_MAGIC = 1.5 * 2.0**23
EXP_CAP = 2.0**62
BIG = 3.0e38

EXP_LN_TABLE = "natural_log_exp_and_others"
SILU_TABLE = "silu_and_others"


def column_layout(D, H):
    at, where = 0, {}
    for name, n in [("dl_b", H // P), ("A_b", H // P), ("B_b", H // P), ("C_b", D // P), ("D_b", D // P),
                    ("conv_b", D // P), ("conv_w0", D // P), ("conv_w1", D // P), ("conv_w2", D // P),
                    ("ln_gamma", D // P), ("ln_beta", D // P)]:
        where[name] = at
        at += n
    return where, at


def build(nc, x, w1T, w2T, w3T, dlT, AT, BT, CT, DT, ffn_w, columns, gamma_row, beta_row, out):
    B, L, D = x.shape
    H = dlT.shape[1]
    CD = D // P
    HD = H // P
    TT = L // P
    XW = D + 2
    assert (CD, HD, TT) == (2, 4, 4) and L == 512 and B % 8 == 0 and B >= 24
    col_at, n_cols = column_layout(D, H)

    x_v = x.rearrange("b (t p) d -> b p t d", p=P)
    out_v = out.rearrange("b (t p) d -> b p t d", p=P)
    ROW = TT * XW
    PITCH = -(-ROW // 64) * 64
    scratch = nc.dram_tensor("x1_scratch", [B, P, PITCH], F32, kind="Internal").ap()

    with ExitStack() as ctx:
        def sb(name, shape, dt=F32):
            return ctx.enter_context(nc.sbuf_tensor(name, shape, dt))

        def sem(name):
            return ctx.enter_context(nc.semaphore(name))

        NAMES = [("w1", CD, D), ("dl", CD, H), ("A", CD, H), ("B", CD, H), ("C", HD, D), ("D", CD, D), ("w2", CD, D),
                 ("w3", CD, D)]
        w_hi = {n: sb(f"{n}_hi", [P, k, o], F32R) for n, k, o in NAMES}
        w_lo = {n: sb(f"{n}_lo", [P, k, o], F32R) for n, k, o in NAMES}
        wq = sb("wq", [P, CD, D], F32R)
        ident = sb("ident", [P, P])
        ones = sb("ones", [P, P])
        neg_half = sb("neg_half", [P, TT])
        cols = sb("cols", [P, n_cols])
        cd_b = sb("cd_b", [P, CD])
        g_row = sb("g_row", [P, D])
        b_row = sb("b_row", [P, D])
        runs = sb("runs", [P, 2 * TT * D + 2 * TT])
        hi_run, lo_run = (runs[:, k * TT * D:(k + 1) * TT * D].rearrange("p (t d) -> p t d", t=TT)
                          for k in range(2))
        scal = sb("scal", [P, 16])

        ext = sb("ext", [P, 2, D])
        x_in = sb("x_in", [P, 2, TT, D])
        x_res = sb("x_res", [P, TT, D])
        x_stat = sb("x_stat", [P, TT, 6])
        x_mv = sb("x_mv", [P, TT, 2])
        x_tmp = sb("x_tmp", [P, 2, TT])
        x_norm = sb("x_norm", [P, 2, TT])
        xn = sb("xn", [P, TT, D])
        xn_hi = sb("xn_hi", [P, CD, L], F32R)
        xn_lo = sb("xn_lo", [P, CD, L], F32R)
        xs = sb("xs", [P, CD, L])
        xs_hi = sb("xs_hi", [P, 2, CD, L], F32R)
        xs_lo = sb("xs_lo", [P, 2, CD, L], F32R)
        temps = sb("temps", [P, 10 * L])

        def temp(k):
            return temps[:, k * 2 * L:(k + 1) * 2 * L].rearrange("p (r l) -> p r l", r=2)

        softp, delta, cumul, gated, hsum = temp(0), temp(1), temp(2), temp(3), temp(4)
        h_hi = sb("h_hi", [P, 2, HD, L], F32R)
        h_lo = sb("h_lo", [P, 2, HD, L], F32R)
        s_buf = sb("s_buf", [P, CD, L])
        s_hi = sb("s_hi", [P, CD, L], F32R)
        s_lo = sb("s_lo", [P, CD, L], F32R)
        gate = sb("gate", [P, CD, L])
        z_buf = sb("z_buf", [P, CD, L])
        z_hi = sb("z_hi", [P, CD, L], F32R)
        z_lo = sb("z_lo", [P, CD, L], F32R)
        x1 = sb("x1", [P, 2, TT, XW])
        x1_stat = sb("x1_stat", [P, TT, 6])
        x1_mv = sb("x1_mv", [P, TT, 2])
        x1_tmp = sb("x1_tmp", [P, 2, TT])
        x1n = sb("x1n", [P, TT, D])

        stage_at, raw = 0, {}
        for name, k, o in NAMES:
            if name == "C":
                raw[name] = x1n[:, :, :].rearrange("p t d -> p (t d)").rearrange("p (k o) -> p k o", k=k)
            else:
                raw[name] = temps[:, stage_at:stage_at + k * o].rearrange("p (k o) -> p k o", k=k)
                stage_at += k * o
        assert stage_at <= 10 * L
        raw_ffn = s_buf

        R1 = 8
        x1_extra = sb("x1_extra", [P, TT, XW])
        x1_in = [temps[:, k * TT * XW:(k + 1) * TT * XW].rearrange("p (t d) -> p t d", t=TT) for k in range(4)]
        x1_in += [x1_extra[:, :, :], x1[:, 0, :, :], x1[:, 1, :, :],
                  runs[:, 0:TT * XW].rearrange("p (t d) -> p t d", t=TT)]
        xn2 = x_in
        xc = [z_buf, gate, s_buf, xs]
        q_hi, q_lo = xs_hi, xs_lo
        y_out = [xn[:, :, :], x_res[:, :, :], x1n[:, :, :],
                 runs[:, TT * XW:TT * XW + TT * D].rearrange("p (t d) -> p t d", t=TT)]

        hb = ctx.enter_context(nc.psum_tensor("hidden_banks", [P, 6, L], F32))
        mb = ctx.enter_context(nc.psum_tensor("misc_banks", [P, 2, L], F32))

        d_x = [sem(f"d_x{r}") for r in range(2)]
        d_store = [sem(f"d_store{r}") for r in range(2)]
        d_x1 = [sem(f"d_x1_{r}") for r in range(8)]
        d_out = [sem(f"d_out{r}") for r in range(4)]
        d_res = sem("d_res")
        d_w = {n: sem(f"d_w_{n}") for n, _, _ in NAMES}
        d_wf, d_cols, d_rows = sem("d_wf"), sem("d_cols"), sem("d_rows")
        g_const = sem("g_const")
        g_xnorm, g_hlo, g_zlo, g_x1stat = (sem(n) for n in ("g_xnorm", "g_hlo", "g_zlo", "g_x1stat"))
        a_whi = sem("a_whi")
        a_xn, a_xnhi, a_tap, a_xs, a_xshi = (sem(n) for n in ("a_xn", "a_xnhi", "a_tap", "a_xs", "a_xshi"))
        a_exp, a_ln, a_decay, a_hhi = (sem(n) for n in ("a_exp", "a_ln", "a_decay", "a_hhi"))
        a_s, a_shi, a_gate, a_zhi, a_x1n = (sem(n) for n in ("a_s", "a_shi", "a_gate", "a_zhi", "a_x1n"))
        p_xT, p_w1, p_dl, p_A, p_B, p_ssm, p_gate, p_mix, p_small = (
            sem(n) for n in ("p_xT", "p_w1", "p_dl", "p_A", "p_B", "p_ssm", "p_gate", "p_mix", "p_small"))
        v_init, v_wlo = sem("v_init"), sem("v_wlo")
        v_xst, v_xag, v_xnlo, v_tap, v_conv, v_xslo = (
            sem(n) for n in ("v_xst", "v_xag", "v_xnlo", "v_tap", "v_conv", "v_xslo"))
        v_cap, v_delta, v_da, v_cum, v_gated, v_h = (
            sem(n) for n in ("v_cap", "v_delta", "v_da", "v_cum", "v_gated", "v_h"))
        v_slo, v_z, v_x1, v_x1st, v_x1ag, v_ext, v_chain = (
            sem(n) for n in ("v_slo", "v_z", "v_x1", "v_x1st", "v_x1ag", "v_ext", "v_chain"))
        a_x1n_last, v_reduced = sem("a_x1n_last"), sem("v_reduced")
        held = sem("held")
        v_chain_w, v_chain_g = sem("v_chain_w"), sem("v_chain_g")
        g_chain_0, g_xa, g_xb, g_x1a, g_x1b = (sem(n) for n in ("g_chain_0", "g_xa", "g_xb", "g_x1a", "g_x1b"))
        q_norm_v, q_norm_a, q_T, q_evac, q_clip, q_hi_s, q_lo_s, q_y, q_fin = (
            sem(n) for n in ("q_norm_v", "q_norm_a", "q_T", "q_evac", "q_clip", "q_hi", "q_lo", "q_y", "q_fin"))

        def col(name, m):
            return cols[:, col_at[name] + m:col_at[name] + m + 1]

        def wait(eng, s, value):
            if isinstance(value, int) and value <= 0:
                return
            eng.wait_ge(s, value)

        def nth(n, r, slots):
            return 16 // slots * (n - r) + 16

        def hold(eng):
            eng.sem_inc(held, 1)

        def absent(n):
            return isinstance(n, int) and not 0 <= n < B

        def first(t):
            return isinstance(t, int) and t == 0

        def last(n):
            return isinstance(n, int) and n == B - 1

        def run_steps(step, eng, between=None):
            for t in range(4):
                step(t, t % 2)
            with eng.Fori(2, B // 2 - 1) as i:
                for u in range(2):
                    step(2 * i + u, u)
            for t in range(B - 2, B + 3):
                step(t, t % 2)
            if between:
                between()
            step(B + 3, 1)

        def run_steps_2(step, eng):
            for t in range(8):
                step(t, t)
            with eng.Fori(1, B // 8 - 1) as i:
                for u in range(8):
                    step(8 * i + u, u)
            for t in range(B - 8, B + 3):
                step(t, t % 8)

        block = ctx.enter_context(nc.Block())

        @block.sync
        def _(sp):
            def load_x(n, r):
                wait(sp, a_xn, n - 1)
                sp.dma_start(x_in[:, r, :, :], x_v[bass.ds(n, 1)].rearrange("o p t d -> (o p) t d")).then_inc(d_x[r], 16)

            sp.dma_start(x_in[:, 0, :, :], x_v[0]).then_inc(d_x[0], 16)
            w_dram = {"w1": w1T, "dl": dlT, "A": AT, "B": BT, "C": CT, "D": DT, "w2": w2T, "w3": w3T}
            for name, _, _ in NAMES:
                sp.dma_start(raw[name], w_dram[name].rearrange("(k p) o -> p k o", p=P)).then_inc(d_w[name], 16)
                if name == "w1":
                    sp.dma_start(cols[:, :], columns).then_inc(d_cols, 16)
                    sp.dma_start(x_in[:, 1, :, :], x_v[1]).then_inc(d_x[1], 16)
            sp.dma_start(raw_ffn[:, :, 0:D], ffn_w.rearrange("(k p) o -> p k o", p=P)).then_inc(d_wf, 16)
            sp.dma_start(g_row[:, :], gamma_row.partition_broadcast(P)).then_inc(d_rows, 16)
            sp.dma_start(b_row[:, :], beta_row.partition_broadcast(P)).then_inc(d_rows, 16)

            def load_residual(n):
                if absent(n):
                    return
                wait(sp, v_x1, 2 * n)
                sp.dma_start(x_res[:, :, :], x_v[bass.ds(n, 1)].rearrange("o p t d -> (o p) t d")).then_inc(d_res, 16)

            def store_x1(n, r):
                if absent(n):
                    return
                sp.wait_ge(g_x1stat, n + 1)
                sp.dma_start(scratch[bass.ds(n, 1), :, 0:ROW].rearrange("o p f -> (o p) f"),
                             x1[:, r, :, :].rearrange("p t d -> p (t d)")).then_inc(d_store[r], 16)

            def step(t, u):
                load_residual(t - 2)
                if not absent(t + 3):
                    load_x(t + 3, 1 - u)
                store_x1(t - 3, 1 - u)

            step(-1, 1)
            for t in range(4):
                step(t, t % 2)
            with sp.Fori(2, B // 2 - 2) as i:
                for u in range(2):
                    step(2 * i + u, u)
            for t in range(B - 4, B + 2):
                step(t, t % 2)

            def load_x1(n, r):
                wait(sp, q_fin, 2 * (n - R1) + 2)
                sp.dma_start(x1_in[r].rearrange("p t d -> p (t d)"),
                             scratch[bass.ds(n, 1), :, 0:ROW].rearrange("o p f -> (o p) f")).then_inc(d_x1[r], 16)

            def store(n, r):
                sp.wait_ge(q_fin, 2 * n + 2)
                sp.dma_start(out_v[bass.ds(n, 1)].rearrange("o p t d -> (o p) t d"), y_out[r]).then_inc(d_out[r], 16)

            sp.wait_ge(g_hlo, HD * B)
            sp.wait_ge(a_hhi, HD * B)
            for n in range(5):
                sp.wait_ge(d_store[n % 2], nth(n, n % 2, 2))
                load_x1(n, n)
            step(B + 2, 0)
            for r in range(2):
                sp.wait_ge(d_store[r], nth(B - 2 + r, r, 2))
            sp.wait_ge(a_x1n_last, TT)
            load_x1(5, 5)
            load_x1(6, 6)
            sp.wait_ge(v_reduced, 2)
            load_x1(7, 7)
            with sp.Fori(0, B // 8 - 1) as i:
                for r in range(8):
                    store(8 * i + r, r % 4)
                    load_x1(8 * i + (r + R1), r)
            for n in range(B - R1, B):
                store(n, n % 4)
            for r in range(4):
                sp.wait_ge(d_out[r], nth(B - 4 + r, r, 4))

        @block.tensor
        def _(pe):
            def product(bank, name, m, x_hi, x_lo, last=True, ready=None):
                kt = w_hi[name].shape[1]
                for k in range(kt):
                    if ready:
                        ready(k)
                    hi = w_hi[name][:, k, m * P:(m + 1) * P]
                    lo = w_lo[name][:, k, m * P:(m + 1) * P]
                    pe.matmul(bank, hi, x_hi[:, k, :], start=(k == 0), stop=False)
                    pe.matmul(bank, hi, x_lo[:, k, :], start=False, stop=False)
                    done = pe.matmul(bank, lo, x_hi[:, k, :], start=False, stop=(last and k == kt - 1))
                return done

            def hidden_product(n, r, j, k):
                if absent(n):
                    return
                q = HD * n + j
                if isinstance(n, int) and n == 0:
                    pe.wait_ge(v_wlo, 2 + k)
                    if j == 1 and k == 2:
                        pe.wait_ge(v_init, 2)
                if k == 0 and j == 0:
                    pe.wait_ge(v_xslo, CD * n + CD)
                wait(pe, (v_delta, v_da, v_gated)[k], q - 1)
                product(hb[:, 3 * (j % 2) + k, :], ("dl", "A", "B")[k], j, xs_hi[:, r], xs_lo[:, r]).then_inc(
                    (p_dl, p_A, p_B)[k], 1)

            def transpose_x(n, c):
                if absent(n):
                    return
                if isinstance(n, int) and n == 0:
                    pe.wait_ge(g_const, 1)
                if c == 0:
                    pe.wait_ge(a_xn, n + 1)
                if absent(n - 3):
                    wait(pe, v_conv, CD * (n - 1) + c + 1)
                else:
                    pe.wait_ge(v_x1, 2 * (n - 3) + c + 1)
                for i in range(TT):
                    done = pe.transpose(mb[:, c, i * P:(i + 1) * P], xn[:, i, c * P:(c + 1) * P], ident[:, :])
                done.then_inc(p_xT, 1)

            def front_product(n, m):
                if absent(n):
                    return
                if isinstance(n, int) and n == 0:
                    pe.wait_ge(v_wlo, 1)
                if m == 0:
                    pe.wait_ge(v_xnlo, CD * n + CD)
                if not absent(n - 2):
                    pe.wait_ge(a_gate, CD * (n - 2) + m + 1)
                product(mb[:, m, :], "w1", m, xn_hi, xn_lo).then_inc(p_w1, 1)

            def skip_product(n, r, m):
                if absent(n):
                    return
                if isinstance(n, int) and n == 0:
                    pe.wait_ge(v_wlo, len(NAMES))
                if absent(n + 2):
                    pe.wait_ge(v_x1, 2 * (n - 1) + m + 1)
                else:
                    pe.wait_ge(v_xnlo, CD * (n + 2) + m + 1)
                product(mb[:, m, :], "D", m, xs_hi[:, r], xs_lo[:, r], last=False)

            def state_product(n, r, m):
                if absent(n):
                    return
                for k in range(HD):
                    if m == 0:
                        pe.wait_ge(a_hhi, HD * n + k + 1)
                        pe.wait_ge(g_hlo, HD * n + k + 1)
                    hi, lo = (w["C"][:, k, m * P:(m + 1) * P] for w in (w_hi, w_lo))
                    pe.matmul(mb[:, m, :], hi, h_hi[:, r, k, :], start=False, stop=False)
                    pe.matmul(mb[:, m, :], hi, h_lo[:, r, k, :], start=False, stop=False)
                    done = pe.matmul(mb[:, m, :], lo, h_hi[:, r, k, :], start=False, stop=(k == HD - 1))
                done.then_inc(p_ssm, 1)

            def gate_product(n, m):
                if absent(n):
                    return

                def ready(k):
                    pe.wait_ge(v_slo, CD * n + k + 1)

                product(mb[:, m, :], "w2", m, s_hi, s_lo, ready=ready if m == 0 else None).then_inc(p_gate, 1)

            def mix(n, half):
                if absent(n):
                    return
                if half == 0:
                    pe.wait_ge(a_s, CD * n + CD)
                if absent(n + 2):
                    pe.wait_ge(a_gate, CD * n + half + 1)
                else:
                    pe.wait_ge(v_conv, CD * (n + 2) + half + 1)
                for e in range(2):
                    for k in range(CD):
                        pe.matmul(mb[:, half, e * D + k * P:e * D + (k + 1) * P],
                                  s_buf[:, k, (2 * half + e) * P:(2 * half + e + 1) * P], ident[:, :],
                                  is_transpose=True, start=(e == 0 and k == 0), stop=True, skip_group_check=True)
                for k in range(CD):
                    if half == 0:
                        pe.wait_ge(a_zhi, CD * n + k + 1)
                        pe.wait_ge(g_zlo, CD * n + k + 1)
                    for e in range(2):
                        acc = mb[:, half, e * D:(e + 1) * D]
                        tok = slice((2 * half + e) * P, (2 * half + e + 1) * P)
                        for z, w in ((z_hi, w_hi), (z_hi, w_lo), (z_lo, w_hi)):
                            done = pe.matmul(acc, z[:, k, tok], w["w3"][:, k, :], start=False, stop=True,
                                             skip_group_check=True)
                done.then_inc(p_mix, 1)

            def step(t, u):
                DL, A, B_ = 0, 1, 2
                hidden_product(t - 1, 1 - u, 0, DL)
                hidden_product(t - 1, 1 - u, 0, A)
                transpose_x(t, 0)
                hidden_product(t - 1, 1 - u, 1, DL)
                hidden_product(t - 1, 1 - u, 1, A)
                hidden_product(t - 1, 1 - u, 0, B_)
                transpose_x(t, 1)
                skip_product(t - 2, u, 0)
                if absent(t - 1):
                    skip_product(t - 2, u, 1)
                state_product(t - 2, u, 0)
                if not absent(t - 1):
                    skip_product(t - 2, u, 1)
                hidden_product(t - 1, 1 - u, 2, DL)
                state_product(t - 2, u, 1)
                hidden_product(t - 1, 1 - u, 3, DL)
                hidden_product(t - 1, 1 - u, 2, A)
                gate_product(t - 2, 0)
                gate_product(t - 2, 1)
                hidden_product(t - 1, 1 - u, 1, B_)
                front_product(t, 0)
                front_product(t, 1)
                hidden_product(t - 1, 1 - u, 3, A)
                hidden_product(t - 1, 1 - u, 2, B_)
                hidden_product(t - 1, 1 - u, 3, B_)
                mix(t - 2, 0)
                mix(t - 2, 1)
                if first(t):
                    ffn_sum()

            def ffn_sum():
                pe.wait_ge(v_init, 1)
                pe.matmul(hb[:, 5, 0:1], ones[:, :], scal[:, 0:1], start=True, stop=True).then_inc(p_small, 1)

            run_steps(step, pe)

            def y_bank(r, half):
                return hb[:, 4 + half, :] if r == 0 else mb[:, half, :]

            def transposes(n, r):
                if absent(n):
                    return
                pe.wait_ge(q_norm_v, n + 1)
                pe.wait_ge(q_norm_a, n + 1)
                wait(pe, q_evac, CD * (n - 1))
                for c in range(CD):
                    for i in range(TT):
                        done = pe.transpose(hb[:, 2 * r + c, i * P:(i + 1) * P], xn2[:, r, i, c * P:(c + 1) * P], ident[:, :])
                    done.then_inc(q_T, 1)

            def projection(n, r):
                if absent(n):
                    return
                pe.wait_ge(q_lo_s, CD * n + CD)
                wait(pe, q_fin, 2 * (n - 1))
                for i in range(TT):
                    acc = y_bank(r, i // 2)[:, (i % 2) * D:(i % 2 + 1) * D]
                    tok = slice(i * P, (i + 1) * P)
                    for k in range(CD):
                        pe.matmul(acc, q_hi[:, r, k, tok], wq[:, k, :], start=(k == 0), stop=False)
                        done = pe.matmul(acc, q_lo[:, r, k, tok], wq[:, k, :], start=False, stop=(k == CD - 1))
                    if i % 2 == 1:
                        done.then_inc(q_y, 1)

            pe.wait_ge(v_gated, HD * B)
            for n in range(2):
                transposes(n, n)
            pe.wait_ge(v_chain, 1)
            pe.transpose(hb[0:1, 4, 0:P], scal[:, 1:2], ident[:, :]).then_inc(p_small, 1)
            pe.wait_ge(v_chain, 2)
            pe.matmul(hb[:, 5, 0:1], ones[0:1, :], scal[0:1, 2:3], start=True, stop=True).then_inc(p_small, 1)
            pe.wait_ge(v_chain, 5)

            def step2(t, u):
                if not first(t):
                    transposes(t + 1, (u + 1) % 2)
                projection(t - 2, u % 2)

            run_steps_2(step2, pe)

        @block.scalar
        def _(act):
            act.preload_act_table_set(EXP_LN_TABLE)

            def split_hi_of(name):
                act.wait_ge(d_w[name], 16)
                act.activation(w_hi[name][:, :, :], raw[name], ACT.Copy).then_inc(a_whi, 1)

            split_hi_of(NAMES[0][0])

            def exp_u(n, j):
                if absent(n):
                    return
                if isinstance(n, int) and n == 0:
                    act.wait_ge(v_wlo, 2)
                act.wait_ge(p_dl, HD * n + j + 1)
                act.activation(softp[:, j % 2, :], hb[:, 3 * (j % 2), :], ACT.Exp, bias=col("dl_b", j)).then_inc(a_exp, 1)

            def ln_1p(n, j):
                if absent(n):
                    return
                act.wait_ge(v_cap, HD * n + j + 1)
                act.activation(softp[:, j % 2, :], softp[:, j % 2, :], ACT.Ln, bias=1.0).then_inc(a_ln, 1)

            def decay(n, j):
                if absent(n):
                    return
                act.wait_ge(v_cum, HD * n + j + 1)
                act.activation(cumul[:, j % 2, :], cumul[:, j % 2, :], ACT.Exp, scale=-1.0).then_inc(a_decay, 1)

            def hidden_hi(n, r, j):
                if absent(n):
                    return
                act.wait_ge(v_h, HD * n + j + 1)
                if j == 0:
                    wait(act, p_ssm, CD * (n - 1))
                act.activation(h_hi[:, r, j, :], hsum[:, j % 2, :], ACT.Copy).then_inc(a_hhi, 1)

            def normalise_x(n, r):
                if absent(n):
                    return
                act.wait_ge(g_xnorm, n + 1)
                wait(act, p_xT, CD * n)
                for i in range(TT):
                    done = act.activation(xn[:, i, :], x_in[:, r, i, :], ACT.Identity, scale=x_norm[:, 0, i:i + 1],
                                          bias=x_norm[:, 1, i:i + 1])
                done.then_inc(a_xn, 1)

            def xn_hi_of(n, c):
                if absent(n):
                    return
                act.wait_ge(p_xT, CD * n + c + 1)
                wait(act, p_w1, CD * n)
                act.activation(xn_hi[:, c, :], mb[:, c, :], ACT.Copy).then_inc(a_xnhi, 1)

            def centre_tap(n, c):
                if absent(n):
                    return
                if isinstance(n, int) and n == 0:
                    act.wait_ge(d_cols, 16)
                act.wait_ge(p_w1, CD * n + c + 1)
                wait(act, v_xslo, CD * (n - 1) + c + 1)
                act.activation(xs[:, c, :], mb[:, c, :], ACT.Identity, scale=col("conv_w1", c),
                               bias=col("conv_b", c)).then_inc(a_tap, 1)

            def silu_x(n, c):
                if absent(n):
                    return
                act.wait_ge(v_conv, CD * n + c + 1)
                act.activation(xs[:, c, :], xs[:, c, :], ACT.Silu).then_inc(a_xs, 1)

            def x_hi_of(n, r, c):
                if absent(n):
                    return
                act.wait_ge(a_xs, CD * n + c + 1)
                wait(act, p_ssm, CD * (n - 1))
                act.activation(xs_hi[:, r, c, :], xs[:, c, :], ACT.Copy).then_inc(a_xshi, 1)

            def ssm_out(n, m, hi):
                if absent(n):
                    return
                if isinstance(n, int) and n == 0:
                    act.wait_ge(v_init, 3)
                act.wait_ge(p_ssm, CD * n + m + 1)
                wait(act, p_mix, 2 * n)
                out_, done = (s_hi, a_shi) if hi else (s_buf, a_s)
                act.activation(out_[:, m, :], mb[:, m, :], ACT.Identity, bias=cd_b[:, m:m + 1]).then_inc(done, 1)

            def silu_gate(n, m):
                if absent(n):
                    return
                act.wait_ge(p_gate, CD * n + m + 1)
                act.activation(gate[:, m, :], mb[:, m, :], ACT.Silu).then_inc(a_gate, 1)

            def z_hi_of(n, m):
                if absent(n):
                    return
                act.wait_ge(v_z, CD * n + m + 1)
                act.activation(z_hi[:, m, :], z_buf[:, m, :], ACT.Copy).then_inc(a_zhi, 1)

            def normalise_x1(n, r):
                if absent(n):
                    return
                act.wait_ge(g_x1stat, n + 1)
                act.wait_ge(v_ext, n + 1)
                for i in range(TT):
                    done = act.activation(x1n[:, i, :], x1[:, r, i, 0:D], ACT.Identity,
                                          scale=x1[:, r, i, D:D + 1], bias=x1[:, r, i, D + 1:D + 2])
                    if last(n):
                        done.then_inc(a_x1n_last, 1)
                if not last(n):
                    done.then_inc(a_x1n, 1)

            normalise_x(0, 0)
            split_hi_of("dl")

            def step(t, u):
                exp_u(t - 1, 0)
                xn_hi_of(t, 0)
                ln_1p(t - 1, 0)
                exp_u(t - 1, 1)
                hidden_hi(t - 2, u, 3)
                xn_hi_of(t, 1)
                if first(t):
                    split_hi_of("A")
                    split_hi_of("B")
                ln_1p(t - 1, 1)
                ssm_out(t - 2, 0, True)
                ssm_out(t - 2, 0, False)
                normalise_x(t + 1, 1 - u)
                decay(t - 1, 0)
                exp_u(t - 1, 2)
                ssm_out(t - 2, 1, False)
                ssm_out(t - 2, 1, True)
                exp_u(t - 1, 3)
                decay(t - 1, 1)
                ln_1p(t - 1, 2)
                ln_1p(t - 1, 3)
                silu = not (absent(t) and absent(t - 2))
                if silu:
                    act.preload_act_table_set(SILU_TABLE)
                silu_gate(t - 2, 0)
                silu_gate(t - 2, 1)
                z_hi_of(t - 2, 0)
                centre_tap(t, 0)
                z_hi_of(t - 2, 1)
                centre_tap(t, 1)
                if first(t):
                    split_hi_of("C")
                silu_x(t, 0)
                silu_x(t, 1)
                x_hi_of(t, u, 0)
                x_hi_of(t, u, 1)
                if first(t):
                    for name in ("D", "w2", "w3"):
                        split_hi_of(name)
                hidden_hi(t - 1, 1 - u, 0)
                hidden_hi(t - 1, 1 - u, 1)
                if silu and not last(t - 2):
                    act.preload_act_table_set(EXP_LN_TABLE)
                decay(t - 1, 2)
                normalise_x1(t - 3, 1 - u)
                decay(t - 1, 3)
                hidden_hi(t - 1, 1 - u, 2)

            def normalise(n, r8):
                if absent(n):
                    return
                i = TT - 1
                act.wait_ge(d_x1[r8], nth(n, r8, 8))
                wait(act, q_T, CD * (n - 1))
                act.activation(xn2[:, r8 % 2, i, :], x1_in[r8][:, i, 0:D], ACT.Identity, scale=x1_in[r8][:, i, D:D + 1],
                               bias=x1_in[r8][:, i, D + 1:D + 2]).then_inc(q_norm_a, 1)

            def evacuate(n, r, r4):
                if absent(n):
                    return
                for c in range(CD):
                    act.wait_ge(q_T, CD * n + c + 1)
                    wait(act, q_lo_s, CD * (n - 4) + c + 1)
                    act.activation(xc[r4][:, c, :], hb[:, 2 * r + c, :], ACT.Identity, scale=scal[:, 6 + c:7 + c],
                                   bias=scal[:, 8 + c:9 + c]).then_inc(q_evac, 1)

            def split_hi(n, r, r4):
                if absent(n):
                    return
                wait(act, q_y, 2 * (n - 1))
                for c in range(CD):
                    act.wait_ge(q_clip, CD * n + c + 1)
                    act.activation(q_hi[:, r, c, :], xc[r4][:, c, :], ACT.Copy).then_inc(q_hi_s, 1)

            run_steps(step, act, between=lambda: (normalise(0, 0), normalise(1, 1)))
            act.wait_ge(v_chain, 4)

            def step2(t, u):
                evacuate(t, u % 2, u % 4)
                if first(t):
                    split_hi(t, 0, 0)
                else:
                    normalise(t + 1, (u + 1) % 8)
                if not first(t - 1):
                    split_hi(t - 1, (u + 1) % 2, (u + 3) % 4)

            run_steps_2(step2, act)

        @block.vector
        def _(dve):
            def raw_f32(ap):
                return ap.bitcast(F32)

            def x_stats(n, r):
                if absent(n):
                    return
                wait(dve, v_xag, n)
                dve.wait_ge(d_x[r], nth(n, r, 2))
                for i in range(TT):
                    done = dve.bn_stats(x_stat[:, i, :], x_in[:, r, i, :])
                done.then_inc(v_xst, 1)

            def x_aggregate(n):
                if absent(n):
                    return
                wait(dve, g_xnorm, n)
                dve.wait_ge(v_xst, n + 1)
                hold(dve)
                for i in range(TT):
                    done = dve.bn_aggr(x_mv[:, i, :], x_stat[:, i, :])
                done.then_inc(v_xag, 1)

            x_stats(0, 0)
            x_aggregate(0)

            def split_weight(k, name):
                dve.wait_ge(a_whi, k + 1)
                dve.tensor_tensor(w_lo[name][:, :, :], raw[name], raw_f32(w_hi[name][:, :, :]), ALU.subtract).then_inc(v_wlo, 1)

            split_weight(0, "w1")
            x_stats(1, 1)
            split_weight(1, "dl")

            def ffn_partial_sums():
                dve.wait_ge(d_wf, 16)
                dve.tensor_reduce(scal[:, 0:1], raw_ffn[:, :, 0:D], AX.XY, ALU.add, apply_absolute_value=True).then_inc(v_init, 1)

            def quantise_ffn():
                dve.wait_ge(p_small, 1)
                dve.tensor_scalar(scal[:, 3:4], hb[:, 5, 0:1], 1.0 / (D * D), None, ALU.mult).then_inc(v_chain_w, 1)
                dve.wait_ge(v_chain_w, 1)
                dve.tensor_scalar(scal[:, 4:5], scal[:, 3:4], Q_EPS, None, ALU.add).then_inc(v_chain_w, 1)
                dve.wait_ge(v_chain_w, 2)
                dve.reciprocal(scal[:, 5:6], scal[:, 4:5]).then_inc(v_chain_w, 1)
                dve.wait_ge(v_chain_w, 3)
                wf = raw_ffn[:, :, 0:D]
                dve.tensor_scalar(wf, wf, scal[:, 5:6], ROUND_MAGIC, ALU.mult, ALU.add).then_inc(v_chain_w, 1)
                dve.wait_ge(v_chain_w, 4)
                dve.tensor_scalar(wf, wf, ROUND_MAGIC, 1.0, ALU.subtract, ALU.min).then_inc(v_chain_w, 1)
                dve.wait_ge(v_chain_w, 5)
                dve.tensor_scalar(wq[:, :, :], wf, -1.0, None, ALU.max).then_inc(v_init, 1)

            def start_values():
                dve.tensor_tensor(cd_b[:, :], cols[:, col_at["C_b"]:col_at["C_b"] + CD],
                                  cols[:, col_at["D_b"]:col_at["D_b"] + CD], ALU.add).then_inc(v_init, 1)
                dve.memset(hi_run[:, :, :], -BIG)
                dve.memset(lo_run[:, :, :], BIG).then_inc(v_ext, 1)

            def cap(n, j):
                if absent(n):
                    return
                q = HD * n + j
                dve.wait_ge(a_exp, q + 1)
                dve.tensor_scalar(softp[:, j % 2, :], softp[:, j % 2, :], EXP_CAP, None, ALU.min).then_inc(v_cap, 1)

            def delta_of(n, j):
                if absent(n):
                    return
                q = HD * n + j
                dve.wait_ge(a_ln, q + 1)
                dve.scalar_tensor_tensor(out=delta[:, j % 2, :], in0=hb[:, 3 * (j % 2), :], scalar=col("dl_b", j),
                                         in1=softp[:, j % 2, :], op0=ALU.add, op1=ALU.max).then_inc(v_delta, 1)

            def delta_A(n, j):
                if absent(n):
                    return
                q = HD * n + j
                dve.wait_ge(p_A, q + 1)
                dve.wait_ge(v_delta, q + 1)
                dve.scalar_tensor_tensor(out=delta[:, j % 2, :], in0=hb[:, 3 * (j % 2) + 1, :], scalar=col("A_b", j),
                                         in1=delta[:, j % 2, :], op0=ALU.add, op1=ALU.mult).then_inc(v_da, 1)

            def decay_sum(n, j):
                if absent(n):
                    return
                dve.wait_ge(v_da, HD * n + j + 1)
                dve.tensor_tensor_scan(out=cumul[:, j % 2, :], data0=delta[:, j % 2, :], data1=delta[:, j % 2, :],
                                       initial=0.0, op0=ALU.add, op1=ALU.bypass).then_inc(v_cum, 1)

            def gated_B(n, j):
                if absent(n):
                    return
                q = HD * n + j
                dve.wait_ge(p_B, q + 1)
                dve.wait_ge(a_decay, q + 1)
                wait(dve, a_hhi, q - 1)
                wait(dve, g_hlo, q - 1)
                dve.scalar_tensor_tensor(out=gated[:, j % 2, :], in0=hb[:, 3 * (j % 2) + 2, :], scalar=col("B_b", j),
                                         in1=cumul[:, j % 2, :], op0=ALU.add, op1=ALU.mult).then_inc(v_gated, 1)

            def hidden_state(n, j):
                if absent(n):
                    return
                dve.wait_ge(v_gated, HD * n + j + 1)
                dve.tensor_tensor_scan(out=hsum[:, j % 2, :], data0=gated[:, j % 2, :], data1=gated[:, j % 2, :],
                                       initial=0.0, op0=ALU.add, op1=ALU.bypass).then_inc(v_h, 1)

            def split_s(n, m):
                if absent(n):
                    return
                dve.wait_ge(a_s, CD * n + m + 1)
                dve.wait_ge(a_shi, CD * n + m + 1)
                dve.tensor_tensor(s_lo[:, m, :], s_buf[:, m, :], raw_f32(s_hi[:, m, :]), ALU.subtract).then_inc(v_slo, 1)

            def extrema(n):
                if absent(n) or last(n):
                    return
                dve.wait_ge(a_x1n, n + 1)
                dve.wait_ge(v_ext, n + 1)
                dve.tensor_tensor(hi_run[:, :, :], hi_run[:, :, :], x1n[:, :, :], ALU.max)
                dve.tensor_tensor(lo_run[:, :, :], lo_run[:, :, :], x1n[:, :, :], ALU.min).then_inc(v_ext, 1)

            def reduce_running(k):
                dve.wait_ge(v_ext, B)
                run, op = ((hi_run, ALU.max), (lo_run, ALU.min))[k]
                dve.tensor_reduce(ext[:, k, :], run[:, :, :].rearrange("p t d -> p d t"), AX.X, op).then_inc(v_reduced, 1)

            def xn_lo_of(n, c):
                if absent(n):
                    return
                dve.wait_ge(a_xnhi, CD * n + c + 1)
                dve.tensor_tensor(xn_lo[:, c, :], mb[:, c, :], raw_f32(xn_hi[:, c, :]), ALU.subtract).then_inc(v_xnlo, 1)

            def left_tap(n, c):
                if absent(n):
                    return
                dve.wait_ge(a_tap, CD * n + c + 1)
                dve.scalar_tensor_tensor(out=xs[:, c, 1:L], in0=mb[:, c, 0:L - 1], scalar=col("conv_w0", c),
                                         in1=xs[:, c, 1:L], op0=ALU.mult, op1=ALU.add).then_inc(v_tap, 1)

            def right_tap(n, c):
                if absent(n):
                    return
                dve.wait_ge(v_tap, CD * n + c + 1)
                dve.scalar_tensor_tensor(out=xs[:, c, 0:L - 1], in0=mb[:, c, 1:L], scalar=col("conv_w2", c),
                                         in1=xs[:, c, 0:L - 1], op0=ALU.mult, op1=ALU.add).then_inc(v_conv, 1)

            def x_lo_of(n, r, c):
                if absent(n):
                    return
                dve.wait_ge(a_xshi, CD * n + c + 1)
                dve.tensor_tensor(xs_lo[:, r, c, :], xs[:, c, :], raw_f32(xs_hi[:, r, c, :]), ALU.subtract).then_inc(v_xslo, 1)

            def gated_ssm(n, m):
                if absent(n):
                    return
                dve.wait_ge(a_gate, CD * n + m + 1)
                dve.wait_ge(a_s, CD * n + m + 1)
                wait(dve, g_zlo, CD * (n - 1) + m + 1)
                wait(dve, a_zhi, CD * (n - 1) + m + 1)
                dve.tensor_tensor(z_buf[:, m, :], gate[:, m, :], s_buf[:, m, :], ALU.mult).then_inc(v_z, 1)

            def add_residual(n, r, half):
                if absent(n):
                    return
                if half == 0:
                    dve.wait_ge(d_res, 16 * n + 16)
                    wait(dve, d_store[r], nth(n - 2, r, 2))
                    wait(dve, a_x1n, n - 1)
                dve.wait_ge(p_mix, 2 * n + half + 1)
                dve.tensor_tensor(x1[:, r, 2 * half:2 * half + 2, 0:D], x_res[:, 2 * half:2 * half + 2, :],
                                  mb[:, half, :].rearrange("p (t d) -> p t d", t=2), ALU.add).then_inc(v_x1, 1)

            def x1_stats(n, r):
                if absent(n):
                    return
                wait(dve, v_x1ag, n)
                dve.wait_ge(v_x1, 2 * n + 2)
                for i in range(TT):
                    done = dve.bn_stats(x1_stat[:, i, :], x1[:, r, i, 0:D])
                done.then_inc(v_x1st, 1)

            def x1_aggregate(n):
                if absent(n):
                    return
                wait(dve, g_x1stat, n)
                dve.wait_ge(v_x1st, n + 1)
                hold(dve)
                for i in range(TT):
                    done = dve.bn_aggr(x1_mv[:, i, :], x1_stat[:, i, :])
                done.then_inc(v_x1ag, 1)

            def step(t, u):
                gated_B(t - 2, 3)
                x_aggregate(t + 1)
                cap(t - 1, 0)
                xn_lo_of(t, 0)
                hidden_state(t - 2, 3)
                x1_stats(t - 3, 1 - u)
                delta_of(t - 1, 0)
                cap(t - 1, 1)
                xn_lo_of(t, 1)
                if first(t):
                    split_weight(2, "A")
                    split_weight(3, "B")
                    ffn_partial_sums()
                    x_stats(2, 0)
                delta_A(t - 1, 0)
                if not first(t):
                    x_stats(t + 2, u)
                delta_of(t - 1, 1)
                split_s(t - 2, 0)
                decay_sum(t - 1, 0)
                delta_A(t - 1, 1)
                x1_aggregate(t - 3)
                decay_sum(t - 1, 1)
                gated_B(t - 1, 0)
                cap(t - 1, 2)
                split_s(t - 2, 1)
                cap(t - 1, 3)
                if not last(t - 3):
                    extrema(t - 4)
                hidden_state(t - 1, 0)
                delta_of(t - 1, 2)
                gated_ssm(t - 2, 0)
                gated_ssm(t - 2, 1)
                gated_B(t - 1, 1)
                delta_A(t - 1, 2)
                left_tap(t, 0)
                left_tap(t, 1)
                right_tap(t, 0)
                right_tap(t, 1)
                if first(t):
                    split_weight(4, "C")
                delta_of(t - 1, 3)
                hidden_state(t - 1, 1)
                x_lo_of(t, u, 0)
                x_lo_of(t, u, 1)
                if first(t):
                    quantise_ffn()
                    for k in range(5, len(NAMES)):
                        split_weight(k, NAMES[k][0])
                    start_values()
                decay_sum(t - 1, 2)
                if last(t - 2):
                    extrema(t - 3)
                add_residual(t - 2, u, 0)
                if last(t - 2):
                    reduce_running(0)
                delta_A(t - 1, 3)
                gated_B(t - 1, 2)
                decay_sum(t - 1, 3)
                hidden_state(t - 1, 2)
                add_residual(t - 2, u, 1)

            def normalise(n, r8):
                if absent(n):
                    return
                r = r8 % 2
                dve.wait_ge(d_x1[r8], nth(n, r8, 8))
                wait(dve, q_T, CD * (n - 1))
                for i in range(TT - 1):
                    done = dve.tensor_scalar(xn2[:, r, i, :], x1_in[r8][:, i, 0:D], x1_in[r8][:, i, D:D + 1],
                                             x1_in[r8][:, i, D + 1:D + 2], ALU.mult, ALU.add)
                done.then_inc(q_norm_v, 1)

            def while_last_norm_is_worked_out():
                reduce_running(1)
                normalise(0, 0)
                normalise(1, 1)

            run_steps(step, dve, between=while_last_norm_is_worked_out)

            count = [0]

            def chained(ins):
                count[0] += 1
                ins.then_inc(v_chain_g, 1)
                dve.wait_ge(v_chain_g, count[0])

            for i in range(TT):
                dve.wait_ge(a_x1n_last, i + 1)
                for k, op in enumerate((ALU.max, ALU.min)):
                    dve.wait_ge(v_reduced, 2 * i + k + 1)
                    dve.tensor_tensor(ext[:, k, :], ext[:, k, :], x1n[:, i, :], op).then_inc(v_reduced, 1)
            dve.wait_ge(v_reduced, 2 * TT + 2)
            dve.wait_ge(d_rows, 32)
            g_rows = g_row[:, :].unsqueeze(1).to_broadcast([P, 2, D])
            b_rows = b_row[:, :].unsqueeze(1).to_broadcast([P, 2, D])
            chained(dve.tensor_tensor(ext[:, :, :], ext[:, :, :], g_rows, ALU.mult))
            chained(dve.tensor_tensor(ext[:, :, :], ext[:, :, :], b_rows, ALU.add))
            dve.tensor_reduce(scal[:, 1:2], ext[:, :, :], AX.XY, ALU.max, apply_absolute_value=True).then_inc(v_chain, 1)
            dve.wait_ge(p_small, 2)
            dve.reduce_max(scal[0:1, 2:3], hb[0:1, 4, 0:P], axis=AX.X).then_inc(v_chain, 1)
            dve.wait_ge(p_small, 3)
            dve.reciprocal(scal[:, 11:12], hb[:, 5, 0:1]).then_inc(v_chain, 1)
            dve.wait_ge(v_chain, 3)
            dve.tensor_scalar(scal[:, 6:10], cols[:, col_at["ln_gamma"]:col_at["ln_gamma"] + 2 * CD],
                              scal[:, 11:12], QB, ALU.mult, ALU.mult).then_inc(v_chain, 1)
            dve.tensor_scalar(scal[:, 13:14], hb[:, 5, 0:1], scal[:, 3:4], 1.0 / QB, ALU.mult, ALU.mult).then_inc(v_chain, 1)

            def clip(n, r4):
                if absent(n):
                    return
                for c in range(CD):
                    dve.wait_ge(q_evac, CD * n + c + 1)
                    dve.tensor_scalar(xc[r4][:, c, :], xc[r4][:, c, :], CLIP, -CLIP, ALU.min, ALU.max).then_inc(q_clip, 1)

            def finish(n, r8):
                if absent(n):
                    return
                r4 = r8 % 4
                wait(dve, d_out[r4], nth(n - 4, r4, 4))
                for half in range(2):
                    dve.wait_ge(q_y, 2 * n + half + 1)
                    src = hb[:, 4 + half, :] if r8 % 2 == 0 else mb[:, half, :]
                    dve.scalar_tensor_tensor(out=y_out[r4][:, 2 * half:2 * half + 2, :], in0=src.rearrange("p (t d) -> p t d", t=2),
                                             scalar=scal[:, 13:14], in1=x1_in[r8][:, 2 * half:2 * half + 2, 0:D],
                                             op0=ALU.mult, op1=ALU.add).then_inc(q_fin, 1)

            dve.wait_ge(v_chain, 5)

            def step2(t, u):
                if not first(t):
                    normalise(t + 1, (u + 1) % 8)
                clip(t, u % 4)
                finish(t - 3, (u + 5) % 8)

            run_steps_2(step2, dve)

        @block.gpsimd
        def _(pool):
            chain = [0]

            def chained(ins):
                chain[0] += 1
                ins.then_inc(g_chain_0, 1)
                pool.wait_ge(g_chain_0, chain[0])

            chained(pool.memset(ident[:, :], 0.0))
            chained(pool.memset(ones[:, :], 1.0))
            chained(pool.memset(neg_half[:, :], -0.5))
            pool.affine_select(out=ident[:, :], in_=ident[:, :], compare_op=ALU.not_equal, fill=1.0, base=0,
                               pattern=[[-1, P]], channel_multiplier=1).then_inc(g_const, 1)

            def x_norm_of(n):
                if absent(n):
                    return
                pool.wait_ge(v_xag, n + 1)
                wait(pool, a_xn, n)
                hold(pool)
                pool.tensor_scalar(x_tmp[:, 0, :], x_mv[:, :, 1], LN_EPS, None, ALU.add).then_inc(g_xa, 1)
                pool.tensor_scalar(x_tmp[:, 1, :], x_mv[:, :, 0], -1.0, 0.0, ALU.mult, ALU.add).then_inc(g_xa, 1)
                pool.wait_ge(g_xa, 2 * n + 2)
                pool.tensor_tensor(x_norm[:, 0, :], x_tmp[:, 0, :], neg_half[:, :], ALU.pow).then_inc(g_xb, 1)
                pool.wait_ge(g_xb, n + 1)
                pool.tensor_tensor(x_norm[:, 1, :], x_tmp[:, 1, :], x_norm[:, 0, :], ALU.mult).then_inc(g_xnorm, 1)

            def x1_norm_of(n, r):
                if absent(n):
                    return
                pool.wait_ge(v_x1ag, n + 1)
                hold(pool)
                pool.tensor_scalar(x1_tmp[:, 0, :], x1_mv[:, :, 1], 1.0 + FFN_LN_EPS, LN_EPS * FFN_LN_EPS,
                                   ALU.mult, ALU.add).then_inc(g_x1a, 1)
                pool.tensor_scalar(x1_tmp[:, 1, :], x1_mv[:, :, 0], -1.0, 0.0, ALU.mult, ALU.add).then_inc(g_x1a, 1)
                pool.wait_ge(g_x1a, 2 * n + 2)
                pool.tensor_tensor(x1[:, r, :, D], x1_tmp[:, 0, :], neg_half[:, :], ALU.pow).then_inc(g_x1b, 1)
                pool.wait_ge(g_x1b, n + 1)
                pool.tensor_tensor(x1[:, r, :, D + 1], x1_tmp[:, 1, :], x1[:, r, :, D], ALU.mult).then_inc(g_x1stat, 1)

            def hidden_lo(n, r, j):
                if absent(n):
                    return
                pool.wait_ge(a_hhi, HD * n + j + 1)
                if j == 0:
                    wait(pool, p_ssm, CD * (n - 1))
                pool.tensor_tensor(h_lo[:, r, j, :], hsum[:, j % 2, :], h_hi[:, r, j, :].bitcast(F32),
                                   ALU.subtract).then_inc(g_hlo, 1)

            def z_lo_of(n, m):
                if absent(n):
                    return
                pool.wait_ge(a_zhi, CD * n + m + 1)
                wait(pool, p_mix, 2 * n)
                pool.tensor_tensor(z_lo[:, m, :], z_buf[:, m, :], z_hi[:, m, :].bitcast(F32), ALU.subtract).then_inc(g_zlo, 1)

            x_norm_of(0)

            def step(t, u):
                x_norm_of(t + 1)
                hidden_lo(t - 2, u, 3)
                x1_norm_of(t - 3, 1 - u)
                z_lo_of(t - 2, 0)
                z_lo_of(t - 2, 1)
                hidden_lo(t - 1, 1 - u, 0)
                hidden_lo(t - 1, 1 - u, 1)
                hidden_lo(t - 1, 1 - u, 2)

            run_steps(step, pool)

            def split_lo(n, r, r4):
                for c in range(CD):
                    pool.wait_ge(q_hi_s, CD * n + c + 1)
                    pool.tensor_tensor(q_lo[:, r, c, :], xc[r4][:, c, :], q_hi[:, r, c, :].bitcast(F32),
                                       ALU.subtract).then_inc(q_lo_s, 1)

            with pool.Fori(0, B // 4) as i:
                for u in range(4):
                    split_lo(4 * i + u, u % 2, u)


def kernel(**inputs):
    import concourse.bacc as _bacc
    from concourse.bass_utils import run_bass_kernel_spmd as _run

    a = {k.split("L0_")[1]: np.asarray(v) for k, v in inputs.items()}
    D, H = a["attn_w1"].shape[0], a["attn_A_w"].shape[0]

    def tiles(v):
        return np.ascontiguousarray(v.reshape(-1, P).T)

    conv = a["attn_conv_w"].reshape(D, 3)
    named = {"dl_b": a["attn_dl_b"], "A_b": a["attn_A_b"], "B_b": a["attn_B_b"], "C_b": a["attn_C_b"],
             "D_b": a["attn_D_b"], "conv_b": a["attn_conv_b"], "conv_w0": conv[:, 0], "conv_w1": conv[:, 1],
             "conv_w2": conv[:, 2], "ln_gamma": a["ffn_ln_gamma"], "ln_beta": a["ffn_ln_beta"]}
    where, _ = column_layout(D, H)
    columns = np.concatenate([tiles(named[n]) for n in where], axis=1)
    arrays = {"x": a["attn_x"], "w1T": a["attn_w1"].T, "w2T": a["attn_w2"].T, "w3T": a["attn_w3"].T,
              "dlT": a["attn_dl_w"].T, "AT": a["attn_A_w"].T, "BT": a["attn_B_w"].T, "CT": a["attn_C_w"].T,
              "DT": a["attn_D_w"].T, "ffn_w": a["ffn_weight"], "columns": columns,
              "gamma_row": a["ffn_ln_gamma"], "beta_row": a["ffn_ln_beta"]}
    arrays = {k: np.ascontiguousarray(v) for k, v in arrays.items()}

    nc = _bacc.Bacc("TRN2", target_bir_lowering=False, num_devices=1)
    args = [nc.dram_tensor(k, v.shape, mybir.dt.from_np(v.dtype), kind="ExternalInput").ap() for k, v in arrays.items()]
    out = nc.dram_tensor("out", a["attn_x"].shape, F32, kind="ExternalOutput").ap()
    build(nc, *args, out)
    r = _run(nc, [arrays], core_ids=[0])
    return r.results[0]["out"]
```
